# Optimizing a Trainium2 kernel written in Bass

```python
import numpy as np
import jax
import jax.numpy as jnp

def _softmax(x, axis=-1):
    return jax.nn.softmax(x, axis=axis)

def _gelu(x):
    return jax.nn.gelu(x, approximate=True)

def _silu(x):
    return jax.nn.silu(x)

def _sigmoid(x):
    return jax.nn.sigmoid(x)

def _layernorm(x, axis=-1, eps=1e-05):
    m = jnp.mean(x, axis=axis, keepdims=True)
    v = jnp.var(x, axis=axis, keepdims=True)
    return (x - m) / jnp.sqrt(v + eps)

def _scatter_add(tgt, idx, src, axis=0):
    return tgt.at[idx].add(src)

def _segment_sum(src, seg, n):
    return jax.ops.segment_sum(src, seg, n)
kernel_name = 'mk_gnn_preln_d2_gnn_r8_4f0a23'

def setup_inputs(seed: int=0):
    np.random.seed(seed)
    _w = jnp.asarray

    def _rec_inputs():
        import jax
        import jax.numpy as jnp
        _gk = jax.random.key(seed)
        x = -0.0003713 + 1 * jax.random.normal(jax.random.fold_in(_gk, 1), (12500, 128), jnp.float32)
        _s = jax.random.randint(jax.random.fold_in(_gk, 2), (100000,), 0, 12500, jnp.int32)
        _d = jax.random.randint(jax.random.fold_in(_gk, 3), (100000,), 0, 12500, jnp.int32)
        _loop = jnp.arange(12500, dtype=jnp.int32)
        src = jnp.concatenate([_s, _d, _loop])
        dst = jnp.concatenate([_d, _s, _loop])
        _o = jnp.argsort(dst, stable=True)
        src = src[_o]
        dst = dst[_o]
        edge_attr_128 = 5.93493e-05 + 1.00006 * jax.random.normal(jax.random.fold_in(_gk, 11), (212500, 128), jnp.float32)
        return (x, src, dst, edge_attr_128)
    x, src, dst, edge_attr_128 = _rec_inputs()

    def _L0_gnn_setup():
        import jax, jax.numpy as jnp
        import numpy as np
        N_NODES = 12500
        N_EDGES = 75000
        H = 128
        key = jax.random.key(seed)
        ks = jax.random.split(key, 8)
        x = jax.random.normal(ks[0], (N_NODES, H), dtype=jnp.float32)
        edge_index = jax.random.randint(ks[1], (2, N_EDGES), 0, N_NODES, dtype=jnp.int64)
        edge_attr = jax.random.normal(ks[2], (N_EDGES, H), dtype=jnp.float32)
        W1 = jax.random.normal(ks[3], (2 * H, 2 * H), dtype=jnp.float32) / np.sqrt(2 * H)
        b1 = jnp.zeros((2 * H,), dtype=jnp.float32)
        gamma = jnp.ones((2 * H,), dtype=jnp.float32)
        beta = jnp.zeros((2 * H,), dtype=jnp.float32)
        prelu_a = jnp.full((1,), 0.25, dtype=jnp.float32)
        W2 = jax.random.normal(ks[4], (2 * H, H), dtype=jnp.float32) / np.sqrt(2 * H)
        b2 = jnp.zeros((H,), dtype=jnp.float32)
        return {'x': x, 'edge_index': edge_index, 'edge_attr': edge_attr, 'W1': W1, 'b1': b1, 'gamma': gamma, 'beta': beta, 'prelu_a': prelu_a, 'W2': W2, 'b2': b2}
    _L0_gnn_all = _L0_gnn_setup()
    _L0_gnn_in = {k: v for k, v in _L0_gnn_all.items() if k in ('W1', 'b1', 'gamma', 'beta', 'prelu_a', 'W2', 'b2')}
    del _L0_gnn_all

    def _L1_gnn_setup():
        import jax, jax.numpy as jnp
        import numpy as np
        N_NODES = 6250
        N_EDGES = 75000
        D_FEAT = 128
        key = jax.random.key(seed)
        k1, k2 = jax.random.split(key)
        x = jax.random.normal(k1, (N_NODES, D_FEAT), dtype=jnp.float32)
        edge_index = jax.random.randint(k2, (2, N_EDGES), 0, N_NODES, dtype=jnp.int64)
        return {'x': x, 'edge_index': edge_index}
    _L1_gnn_all = _L1_gnn_setup()
    _L1_gnn_in = {k: v for k, v in _L1_gnn_all.items() if k in ()}
    del _L1_gnn_all
    return {'x': x, 'src': src, 'dst': dst, 'edge_attr_128': edge_attr_128, 'L0_gnn_W1': _L0_gnn_in['W1'], 'L0_gnn_b1': _L0_gnn_in['b1'], 'L0_gnn_gamma': _L0_gnn_in['gamma'], 'L0_gnn_beta': _L0_gnn_in['beta'], 'L0_gnn_prelu_a': _L0_gnn_in['prelu_a'], 'L0_gnn_W2': _L0_gnn_in['W2'], 'L0_gnn_b2': _L0_gnn_in['b2']}

def reference(x, src, dst, edge_attr_128, L0_gnn_W1, L0_gnn_b1, L0_gnn_gamma, L0_gnn_beta, L0_gnn_prelu_a, L0_gnn_W2, L0_gnn_b2):
    import jax
    import jax.numpy as jnp

    def _L0_gnn_ref(x, edge_index, edge_attr, W1, b1, gamma, beta, prelu_a, W2, b2):
        import jax, jax.numpy as jnp
        import numpy as np
        N_NODES = 12500
        N_EDGES = 75000
        H = 128
        n = x.shape[0]
        col = edge_index[1]
        summed = jax.ops.segment_sum(edge_attr, col, num_segments=n)
        cnt = jax.ops.segment_sum(jnp.ones((edge_attr.shape[0],), edge_attr.dtype), col, num_segments=n)
        agg = summed / jnp.maximum(cnt, 1.0)[:, None]
        h = jnp.concatenate([x, agg], axis=1)
        h = h @ W1 + b1
        mu = jnp.mean(h, axis=-1, keepdims=True)
        var = jnp.mean(jnp.square(h - mu), axis=-1, keepdims=True)
        h = (h - mu) * jax.lax.rsqrt(var + 1e-05) * gamma + beta
        h = jnp.where(h >= 0, h, prelu_a[0] * h)
        return h @ W2 + b2

    def _L1_gnn_ref(x, edge_index):
        import jax, jax.numpy as jnp
        import numpy as np
        N_NODES = 6250
        N_EDGES = 75000
        D_FEAT = 128
        n = x.shape[0]
        src = edge_index[0]
        dst = edge_index[1]
        deg = jax.ops.segment_sum(jnp.ones(src.shape[0], dtype=x.dtype), dst, num_segments=n)
        deg_inv_sqrt = jnp.where(deg > 0, jax.lax.rsqrt(jnp.maximum(deg, 1.0)), 0.0)
        norm = deg_inv_sqrt[src] * deg_inv_sqrt[dst]
        msg = x[src] * norm[:, None]
        out = jax.ops.segment_sum(msg, dst, num_segments=n)
        return out
    edge_index = jnp.stack([src, dst])
    h = jnp.maximum(_layernorm(x, axis=-1), 0.0)
    x = x + _L0_gnn_ref(h, edge_index, edge_attr_128, L0_gnn_W1, L0_gnn_b1, L0_gnn_gamma, L0_gnn_beta, L0_gnn_prelu_a, L0_gnn_W2, L0_gnn_b2)
    h = jnp.maximum(_layernorm(x, axis=-1), 0.0)
    x = x + _L1_gnn_ref(h, edge_index)
    return x

_drawn_inputs = setup_inputs


def setup_inputs(seed=0):
    import zlib

    import numpy as np

    out = dict(_drawn_inputs(seed))
    spreads = {'L0_gnn_b1': (0.0, 0.1),
     'L0_gnn_gamma': (1.0, 0.2),
     'L0_gnn_beta': (0.0, 0.1),
     'L0_gnn_b2': (0.0, 0.1)}
    factors = {}
    for name, (base, spread) in spreads.items():
        noise = np.random.default_rng([zlib.crc32(name.encode()), seed]).standard_normal(out[name].shape)
        drawn = base * np.exp(spread * noise) if base else spread * noise
        out[name] = jnp.asarray(drawn.astype(out[name].dtype))
    for name, factor in factors.items():
        out[name] = (out[name] * factor).astype(out[name].dtype)
    return out
```

```python
from contextlib import ExitStack

import concourse.bass as bass
from concourse import mybir

F32 = mybir.dt.float32
BF16 = mybir.dt.bfloat16
I32 = mybir.dt.int32
ALU = mybir.AluOpType
ACT = mybir.ActivationFunctionType
AX_X = mybir.AxisListType.X

P = 128
T = 7
R = 2
RT = R * T
W = 64
RING = 4
NT = 2
PER = 4
EPS = 1e-5
PAD = -(1 << 20)


def gnn_kernel(nc, x, src, dst, attr, W1, b1, gamma, beta, prelu_a, W2, b2, table, x1_dram, out):
    N, H = x.shape
    E = attr.shape[0]
    F = W1.shape[1]
    assert H == P and F == 2 * P and W1.shape[0] == 2 * P
    GE = T * P
    CE = R * GE
    NC = -(-E // CE)
    LAST = E - (NC - 1) * CE
    assert NC <= P and GE < LAST and NC >= 2 * RING
    NK = -(-N // (NT * P))
    NTILES = NK * NT
    NPAD = NTILES * P + W
    TAIL = N - (NTILES - 1) * P
    assert 0 < TAIL <= P and NK >= 3 * PER
    SE = E // P
    SREST = E % P

    with ExitStack() as ctx:
        def sb(name, shape, dt=F32):
            return ctx.enter_context(nc.sbuf_tensor(name, shape, dt))

        def bank(name, shape):
            return ctx.enter_context(nc.psum_tensor(name, shape, F32))

        def sem(name):
            return ctx.enter_context(nc.semaphore(name))

        acc = sb("acc", [P, NPAD])
        cnt = sb("cnt", [1, NPAD])
        rows = sb("rows", [P, RING, RT, P])
        local = sb("local", [P, NC, RT])
        source = sb("source", [P, NC, RT], I32)
        hot = sb("hot", [P, 2, RT, W])
        assert RT * W * 2 >= CE
        inside = hot[:].rearrange("p b t w -> p (b t w)")[:, 0:CE]
        raw = sb("raw", [P, CE], I32)
        rawf = sb("rawf", [P, CE])
        first = sb("first", [P, R])
        first_row = sb("first_row", [1, NC * R], I32)
        good = sb("good", [P, 1])
        flag = sb("flag", [1, 1], I32)
        index = sb("index", [P, RING, RT], I32)
        ident = sb("ident", [P, P])
        iota_i = sb("iota_i", [P, W], I32)
        ones = sb("ones", [P, 1])
        zeros = sb("zeros", [P, NT * P])
        ones_b = sb("ones_b", [P, P], BF16)
        eps = sb("eps", [P, 1])
        w1 = sb("w1", [P, 2, F])
        w2 = sb("w2", [P, 2, P])
        bias = sb("bias", [P, F + P])
        bias_rest = sb("bias_rest", [P, F + P])
        bias_hi = sb("bias_hi", [P, F + P], BF16)
        bias_mid = sb("bias_mid", [P, F + P], BF16)
        bias_parts = sb("bias_parts", [P, F + P], BF16)
        gb = sb("gb", [P, 2, 2])
        gbn = sb("gbn", [P, 2, 2])
        slope = sb("slope", [P, 2])
        inv_cnt = sb("inv_cnt", [P, NTILES])
        deg_is = sb("deg_is", [P, NTILES])
        cnt1 = sb("cnt1", [P, NTILES])
        cnt_sd = sb("cnt_sd", [P, NTILES])
        cnt_any = sb("cnt_any", [P, NTILES])
        xin = sb("xin", [P, PER, NT, P])
        agg = sb("agg", [P, 2, NT, P])
        hb = sb("hb", [P, 2, NT, P])
        hT = sb("hT", [P, 2, NT, P])
        pre = sb("pre", [P, NT, F])
        mid = sb("mid", [P, NT, F])
        midn = sb("midn", [P, NT, F])
        pos = sb("pos", [P, 2, NT, P])
        neg = sb("neg", [P, 2, NT, P])
        act_t = sb("act_t", [P, 2, NT, P])
        x1 = sb("x1", [P, 2, NT, P])
        h2 = sb("h2", [P, 2, NT, P])
        stats = sb("stats", [P, 3, NT, 6])
        mv = sb("mv", [P, 3, NT, 2])
        sd = sb("sd", [P, 3, NT])
        rstd = sb("rstd", [P, 3, NT])
        nb = sb("nb", [P, 3, NT])
        slow_dst = sb("slow_dst", [1, P], I32)
        slow_src = sb("slow_src", [P, 1], I32)

        p_iota = bank("p_iota", [P, 512])
        p_win = [bank(f"p_win{i}", [P, 512]) for i in range(2)]
        p_hT = bank("p_hT", [P, 512])
        p_pre = bank("p_pre", [P, 512])
        p_agg = bank("p_agg", [P, 512])
        p_mT = bank("p_mT", [P, 512])
        p_out = bank("p_out", [P, 512])
        iota = p_iota[:, 0:W]

        def p_cnt(u):
            return p_win[u % 2][0:1, R * W:2 * R * W]

        block = ctx.enter_context(nc.Block())

        s_raw = sem("raw_in")
        s_raw_set = sem("raw_filled")
        s_first = sem("first_row_in")
        s_const = sem("weights_in")
        s_pool_const = sem("pool_consts")
        s_ones = sem("ones_ready")
        s_gbn = sem("bias_parts_ready")
        s_rawf = sem("raw_as_float")
        s_final = [sem(f"sums{l}_final") for l in range(2)]
        s_agg = sem("agg_copied")
        s_agg2 = sem("agg2_copied")
        s_turned = sem("raw_turned")
        s_local = sem("local_ready")
        s_source = sem("source_ready")
        s_good = sem("good_summed")
        s_flag = sem("flag_ready")
        s_acc0 = sem("acc_zeroed")
        s_rows = [[sem(f"rows{l}_in{i}") for i in range(RING)] for l in range(2)]
        s_index = sem("index_ready")
        s_hot = [sem(f"hot{l}_ready") for l in range(2)]
        s_win = [sem(f"window{l}_summed") for l in range(2)]
        s_add = [sem(f"window{l}_added") for l in range(2)]
        s_cntT = sem("counts_turned")
        s_cnt1 = sem("counts_clamped")
        s_csd = sem("counts_sqrt")
        s_deg = sem("degrees_ready")
        s_x = [sem(f"x_in{i}") for i in range(PER)]
        s_var = sem("x_stats")
        s_sd = sem("x_sd")
        s_nb = sem("x_scale")
        s_h = sem("h_ready")
        s_hTp = sem("h_turned")
        s_hT = sem("h_copied")
        s_pre = sem("linear1_done")
        s_prec = sem("linear1_copied")
        s_mid = sem("mid_stats")
        s_midsd = sem("mid_sd")
        s_midn = sem("mid_normed")
        s_mT = sem("mid_turned")
        s_pn = sem("relus_ready")
        s_act = sem("prelu_ready")
        s_out = sem("linear2_done")
        s_x1 = sem("x1_stats")
        s_x1sd = sem("x1_sd")
        s_x1nb = sem("x1_scale")
        s_h2 = sem("h2_ready")
        s_x1st = [sem(f"x1_stored{i}") for i in range(PER)]
        s_h2st = [sem(f"h2_stored{i}") for i in range(PER)]
        s_clear = sem("acc_cleared")
        s_chain = sem("dve_chain")
        s_links = [sem(f"dve_{n}_chain") for n in ("x", "mid", "x1")]
        s_xl = [sem(f"x1_in{i}") for i in range(PER)]
        s_fT = sem("sums_turned")
        s_f = sem("result_ready")
        s_st = [sem(f"result_stored{i}") for i in range(PER)]
        s_g0 = [sem(f"general{l}_zeroed") for l in range(2)]
        s_gd = [sem(f"general{l}_dst_in") for l in range(2)]
        s_gi = sem("general_src_in")
        s_gr = [sem(f"general{l}_rows_in") for l in range(2)]
        s_gt = [sem(f"general{l}_turned") for l in range(2)]
        s_ga = [sem(f"general{l}_added") for l in range(2)]
        s_ge = [sem(f"general{l}_edge") for l in range(2)]

        def wait(eng, s, value):
            if not isinstance(value, int) or value > 0:
                eng.wait_ge(s, value)

        def chunks(eng, step):
            for u in range(RING):
                step(0, u)
            whole = NC // RING
            with eng.Fori(1, whole) as i:
                for u in range(RING):
                    step(i, u)
            for u in range(NC - whole * RING):
                step(whole, u)

        def node_steps(eng, step, drain=0):
            for u in range(PER):
                step(0, u)
            with eng.Fori(1, NK // PER) as i:
                for u in range(PER):
                    step(i, u)
            for k in range(NK - NK % PER, NK + drain):
                step(k // PER, k % PER)

        def before(i, u, back, period=PER):
            return i + (u - back) // period, (u - back) % period

        def is_step(i, u, back):
            return not isinstance(i, int) or 0 <= i * PER + u - back < NK

        def turns(u):
            return (NK - 1 - u) // PER + 1

        def general(eng):
            eng.wait_ge(s_flag, 1)
            return eng.value_load(flag[0:1, 0:1], min_val=0, max_val=1)

        attr_c = attr[0:(NC - 1) * CE].rearrange("(c r p t) h -> c p r (t h)", r=R, p=P, t=T)

        def load_rows(eng, i, u):
            c = i * RING + u
            wait(eng, s_win[0], c - RING + 1)
            place = rows[:, u].rearrange("p (r t) h -> p r (t h)", r=R)
            if isinstance(c, int) and c == NC - 1:
                e = c * CE
                rest = LAST - GE
                eng.dma_start(place[:, 0], attr[e:e + GE].rearrange("(p t) h -> p (t h)", t=T)).then_inc(s_rows[0][u], 16)
                e += GE
                full = rest // T
                if full:
                    eng.dma_start(place[0:full, 1], attr[e:e + full * T].rearrange("(p t) h -> p (t h)", t=T)).then_inc(
                        s_rows[0][u], 16)
                if rest % T:
                    eng.dma_start(place[full:full + 1, 1, 0:(rest % T) * P],
                                  attr[e + full * T:e + rest].rearrange("(p t) h -> p (t h)", p=1)).then_inc(s_rows[0][u], 16)
            else:
                src_ap = attr_c[c] if isinstance(c, int) else attr_c[bass.ds(c, 1)].rearrange("c p r th -> (c p) r th")
                eng.dma_start(place, src_ap).then_inc(s_rows[0][u], 16)

        rest_ = LAST - GE
        LAST_DMAS = 1 + (1 if rest_ // T else 0) + (1 if rest_ % T else 0)

        @block.sync
        def _(sp):
            body = (NC - 1) * CE
            sp.wait_ge(s_raw_set, 1)
            sp.dma_start(raw[0:NC - 1, :], dst[0:body].rearrange("(c e) -> c e", e=CE)).then_inc(s_raw, 16)
            sp.dma_start(raw[NC - 1:NC, 0:LAST], dst[body:E].rearrange("(c e) -> c e", c=1)).then_inc(s_raw, 16)
            with nc.allow_non_contiguous_dma(reason="one value of each group"):
                whole = GE * (NC * R - 1)
                sp.dma_start(first_row[0:1, 0:NC * R - 1], dst[0:whole].rearrange("(g e) -> e g", e=GE)[0:1, :]).then_inc(s_first, 16)
                sp.dma_start(first_row[0:1, NC * R - 1:NC * R], dst[whole:whole + 1].rearrange("(g e) -> e g", e=1)).then_inc(s_first, 16)
            sp.wait_ge(s_raw_set, 2)
            sp.dma_start(raw[0:NC - 1, :], src[0:body].rearrange("(c e) -> c e", e=CE)).then_inc(s_raw, 16)
            sp.dma_start(raw[NC - 1:NC, 0:LAST], src[body:E].rearrange("(c e) -> c e", c=1)).then_inc(s_raw, 16)

            chunks(sp, lambda i, u: load_rows(sp, i, u))

            with sp.If(general(sp) > 0):
                def slow_tile(t, n, k):
                    sp.wait_ge(s_ga[0], k + 1)
                    e = t * P
                    sp.dma_start(slow_dst[0:1, 0:n], dst[bass.ds(e, n)].rearrange("(a e) -> a e", a=1)).then_inc(s_gd[0], 16)
                    sp.dma_start(rows[0:n, 0, 0, :], attr[bass.ds(e, n)]).then_inc(s_gr[0], 16)
                with sp.Fori(0, SE) as t:
                    slow_tile(t, P, t)
                if SREST:
                    slow_tile(SE, SREST, SE)

            def node_rows(dram, k):
                return dram[bass.ds(k * (NT * P), NT * P)].rearrange("(j p) h -> p j h", p=P)

            def load_x(i, u):
                k = i * PER + u
                wait(sp, s_x1, k - PER + 1)
                if isinstance(k, int) and k == NK - 1:
                    for j in range(NT):
                        n, m = (k * NT + j) * P, P if j < NT - 1 else TAIL
                        sp.dma_start(xin[0:m, u, j], x[n:n + m]).then_inc(s_x[u], 16)
                else:
                    sp.dma_start(xin[:, u], node_rows(x, k)).then_inc(s_x[u], 16)

            def store_nodes(i, u):
                k = i * PER + u
                sp.wait_ge(s_h2, k + 1)
                sp.dma_start(node_rows(table, k), h2[:, u % 2]).then_inc(s_h2st[u], 16)
                sp.dma_start(node_rows(x1_dram, k), x1[:, u % 2]).then_inc(s_x1st[u], 16)

            def node_step(i, u):
                if is_step(i, u, 0):
                    load_x(i, u)
                if is_step(i, u, 3):
                    store_nodes(*before(i, u, 3))
            node_steps(sp, node_step, 3)

            with sp.If(general(sp) > 0):
                def slow_tile(t, n, k):
                    sp.wait_ge(s_ga[1], k + 1)
                    sp.dma_start(slow_dst[0:1, 0:n], dst[bass.ds(t * P, n)].rearrange("(a e) -> a e", a=1)).then_inc(s_gd[1], 16)
                    sp.dma_start(slow_src[0:n, :], src[bass.ds(t * P, n)].rearrange("(e a) -> e a", a=1)).then_inc(s_gi, 16)
                with sp.Fori(0, SE) as t:
                    slow_tile(t, P, t)
                if SREST:
                    slow_tile(SE, SREST, SE)

            for u in range(PER):
                sp.wait_ge(s_x1st[u], 16 * turns(u))

            def load_x1(i, u):
                k = i * PER + u
                wait(sp, s_f, k - PER + 1)
                sp.dma_start(xin[:, u], node_rows(x1_dram, k)).then_inc(s_xl[u], 16)

            def store_out(i, u):
                k = i * PER + u
                sp.wait_ge(s_f, k + 1)
                if isinstance(k, int) and k == NK - 1:
                    for j in range(NT):
                        n, m = (k * NT + j) * P, P if j < NT - 1 else TAIL
                        sp.dma_start(out[n:n + m], x1[0:m, u % 2, j]).then_inc(s_st[u], 16)
                else:
                    sp.dma_start(node_rows(out, k), x1[:, u % 2]).then_inc(s_st[u], 16)

            def last_step(i, u):
                if is_step(i, u, 0):
                    load_x1(i, u)
                if is_step(i, u, 3):
                    store_out(*before(i, u, 3))
            node_steps(sp, last_step, 3)
            for u in range(PER):
                sp.wait_ge(s_st[u], 16 * (turns(u) + (NT - 1 if u == (NK - 1) % PER else 0)))

        @block.gpsimd
        def _(pool):
            pool.memset(ident[:], 0.0).then_inc(s_pool_const, 1)
            pool.wait_ge(s_pool_const, 1)
            pool.affine_select(out=ident[:], in_=ident[:], compare_op=ALU.not_equal, fill=1.0, base=0,
                               pattern=[[-1, P]], channel_multiplier=1).then_inc(s_pool_const, 1)
            pool.iota(iota_i[:], pattern=[[1, W]], base=0, channel_multiplier=0).then_inc(s_pool_const, 1)
            pool.memset(zeros[:], 0.0)
            pool.memset(acc[:], 0.0).then_inc(s_acc0, 1)

            pool.wait_ge(s_final[0], 1)

            def move_agg(i, u):
                k = i * PER + u
                wait(pool, s_pre, k - 1)
                part = acc[:, bass.ds(k * (NT * P), NT * P)]
                pool.tensor_copy(agg[:, u % 2].rearrange("p j h -> p (j h)"), part).then_inc(s_agg, 1)
                pool.wait_ge(s_agg, k + 1)
                pool.nop(nofuse=True)
                pool.tensor_copy(part, zeros[:]).then_inc(s_clear, 1)
            node_steps(pool, move_agg)

            for u in range(PER):
                pool.wait_ge(s_h2st[u], 16 * turns(u))

            def gather(i, u):
                c = i * RING + u
                pool.wait_ge(s_index, c + 1)
                wait(pool, s_win[1], c - RING + 1)
                pool.nop(nofuse=True)
                for t in range(RT):
                    pool.indirect_dma_start(rows[:, u, t], None, table, bass.IndirectOffsetOnAxis(ap=index[:, u, t:t + 1], axis=0)).then_inc(s_rows[1][u], 16)
            chunks(pool, gather)

            with pool.If(general(pool) > 0):
                def slow_tile(n, k):
                    pool.wait_ge(s_gi, 16 * k + 16)
                    pool.nop(nofuse=True)
                    pool.indirect_dma_start(rows[0:n, 0, 0, :], None, table, bass.IndirectOffsetOnAxis(ap=slow_src[0:n, 0:1], axis=0)).then_inc(s_gr[1], 16)
                with pool.Fori(0, SE) as t:
                    slow_tile(P, t)
                if SREST:
                    slow_tile(SREST, SE)

        @block.scalar
        def _(act):
            act.dma_start(w1[:], W1.rearrange("(a p) f -> p a f", p=P)).then_inc(s_const, 16)
            act.dma_start(w2[:], W2.rearrange("(a p) h -> p a h", p=P)).then_inc(s_const, 16)
            act.dma_start(bias[:, 0:F], b1.rearrange("(a f) -> a f", a=1).to_broadcast([P, F])).then_inc(s_const, 16)
            act.dma_start(bias[:, F:F + P], b2.rearrange("(a f) -> a f", a=1).to_broadcast([P, P])).then_inc(s_const, 16)
            with nc.allow_non_contiguous_dma(reason="512 single values"):
                act.dma_start(gb[:, 0, :], gamma.rearrange("(a p) -> p a", p=P)).then_inc(s_const, 16)
                act.dma_start(gb[:, 1, :], beta.rearrange("(a p) -> p a", p=P)).then_inc(s_const, 16)
            act.dma_start(slope[:, 0:1], prelu_a.rearrange("(a f) -> a f", a=1).to_broadcast([P, 1])).then_inc(s_const, 16)

            act.wait_ge(s_ones, 1)
            act.wait_ge(s_cnt1, 1)
            act.activation(cnt_sd[:], cnt1[:], ACT.Sqrt).then_inc(s_csd, 1)

            def norm_x(i, u):
                k = i * PER + u
                act.wait_ge(s_var, k + 1)
                act.activation(sd[:, 0], mv[:, 0, :, 1], ACT.Sqrt, bias=eps[:, 0:1]).then_inc(s_sd, 1)
                act.wait_ge(s_nb, k + 1)
                wait(act, s_hTp, k - 1)
                for j in range(NT):
                    last = act.activation(hb[:, u % 2, j], xin[:, u, j], ACT.Relu, scale=rstd[:, 0, j:j + 1], bias=nb[:, 0, j:j + 1])
                last.then_inc(s_h, 1)
                act.wait_ge(s_hTp, k + 1)
                wait(act, s_pre, k - 1)
                act.copy(hT[:, u % 2], p_hT[:, 0:NT * P].rearrange("p (j h) -> p j h", j=NT)).then_inc(s_hT, 1)

            def copy_pre(i, u):
                k = i * PER + u
                act.wait_ge(s_pre, k + 1)
                wait(act, s_midn, k)
                act.copy(pre[:], p_pre[:, :].rearrange("p (j f) -> p j f", j=NT)).then_inc(s_prec, 1)
                act.wait_ge(s_mid, k + 1)
                act.activation(sd[:, 1], mv[:, 1, :, 1], ACT.Sqrt, bias=eps[:, 0:1]).then_inc(s_midsd, 1)

            def relus(i, u):
                k = i * PER + u
                act.wait_ge(s_mT, k + 1)
                wait(act, s_act, k)
                for a in range(2):
                    t = p_mT[:, a * NT * P:(a + 1) * NT * P].rearrange("p (j h) -> p j h", j=NT)
                    act.activation(pos[:, a], t, ACT.Relu, scale=gb[:, 0, a:a + 1], bias=gb[:, 1, a:a + 1])
                    last = act.activation(neg[:, a], t, ACT.Relu, scale=gbn[:, 0, a:a + 1], bias=gbn[:, 1, a:a + 1])
                last.then_inc(s_pn, 1)

            def norm_x1(i, u):
                k = i * PER + u
                act.wait_ge(s_x1, k + 1)
                act.activation(sd[:, 2], mv[:, 2, :, 1], ACT.Sqrt, bias=eps[:, 0:1]).then_inc(s_x1sd, 1)
                act.wait_ge(s_x1nb, k + 1)
                i2, u2 = before(i, u, 2)
                wait(act, s_h2st[u2], i2 * 16 + 16)
                for j in range(NT):
                    last = act.activation(h2[:, u % 2, j], x1[:, u % 2, j], ACT.Relu, scale=rstd[:, 2, j:j + 1], bias=nb[:, 2, j:j + 1])
                last.then_inc(s_h2, 1)

            act.wait_ge(s_gbn, 1)
            def node_step(i, u):
                if is_step(i, u, 1):
                    copy_pre(*before(i, u, 1))
                if is_step(i, u, 0):
                    norm_x(i, u)
                if is_step(i, u, 2):
                    relus(*before(i, u, 2))
                    norm_x1(*before(i, u, 2))
            node_steps(act, node_step, 2)

            act.wait_ge(s_source, 1)

            def copy_index(i, u):
                if not isinstance(i, int) or i > 0:
                    act.wait_ge(s_rows[1][u], i * (16 * RT))
                act.copy(index[:, u], source[:, bass.ds(i * RING + u, 1), :].rearrange("p c t -> p (c t)")).then_inc(s_index, 1)
            chunks(act, copy_index)

            act.wait_ge(s_final[1], 1)

            def move_sums(i, u):
                k = i * PER + u
                wait(act, s_fT, k - 1)
                act.copy(agg[:, u % 2].rearrange("p j h -> p (j h)"), acc[:, bass.ds(k * (NT * P), NT * P)]).then_inc(s_agg2, 1)
            node_steps(act, move_sums)

        @block.tensor
        def _(pe):
            banks = [p_hT, p_pre, p_agg, p_mT]

            def turn_raw():
                for rt in range(RT):
                    r, t = rt // T, rt % T
                    v = rawf[0:NC, r * GE:(r + 1) * GE].rearrange("c (p t) -> c t p", t=T)[:, t, :]
                    last = pe.transpose(banks[rt // 4][:, (rt % 4) * P:(rt % 4) * P + NC], v, ident[0:NC, 0:NC])
                last.then_inc(s_turned, 1)

            pe.wait_ge(s_pool_const, 2)
            pe.wait_ge(s_rawf, 1)
            turn_raw()
            pe.wait_ge(s_good, 1)
            pe.matmul(p_out[0:1, 0:1], good[0:NC, 0:1], ones[0:NC, 0:1], start=True, stop=True).then_inc(s_good, 1)
            pe.wait_ge(s_rawf, 2)
            pe.wait_ge(s_local, 1)
            turn_raw()

            def sums(layer):
                def step(i, u):
                    c = i * RING + u
                    lastc = isinstance(c, int) and c == NC - 1
                    pe.wait_ge(s_hot[layer], c + 1)
                    if layer == 0:
                        pe.wait_ge(s_rows[0][u], i * 16 + (16 * LAST_DMAS if lastc else 16))
                        wait(pe, s_add[0], (c - 1) * 4)
                    else:
                        pe.wait_ge(s_rows[1][u], i * (16 * RT) + 16 * RT)
                        wait(pe, s_add[1], (c - 1) * R)
                    win = p_win[u % 2]
                    for rt in range(RT):
                        r, t = rt // T, rt % T
                        last = pe.matmul(win[:, r * W:(r + 1) * W], rows[:, u, rt], hot[:, u % 2, rt], start=(t == 0), stop=(t == T - 1))
                    if layer == 0:
                        for rt in range(RT):
                            r, t = rt // T, rt % T
                            ones_of = hot[:, u % 2, rt].bitcast(BF16).rearrange("p (w e) -> p w e", e=2)[:, :, 1]
                            last = pe.matmul(p_cnt(u)[:, r * W:(r + 1) * W], ones_b[:, 0:1], ones_of, start=(t == 0), stop=(t == T - 1))
                    last.then_inc(s_win[layer], 1)
                chunks(pe, step)

            def general_sums(layer):
                with pe.If(general(pe) > 0):
                    def slow_tile(n, k):
                        pe.wait_ge(s_gr[layer], 16 * k + 16)
                        pe.wait_ge(s_ga[layer], k + 1)
                        pe.transpose(p_hT[:, 0:n], rows[0:n, 0, 0, :], ident[0:n, 0:n]).then_inc(s_gt[layer], 1)
                    with pe.Fori(0, SE) as t:
                        slow_tile(P, t)
                    if SREST:
                        slow_tile(SREST, SE)

            pe.wait_ge(s_ones, 1)
            sums(0)
            general_sums(0)

            pe.wait_ge(s_final[0], 1)
            for b in range(NTILES):
                last = pe.matmul(p_agg[:, b:b + 1], cnt[0:1, b * P:(b + 1) * P], ones[0:1, 0:1], start=True, stop=True)
            last.then_inc(s_cntT, 1)
            pe.wait_ge(s_deg, 1)
            pe.wait_ge(s_gbn, 1)
            pe.wait_ge(s_const, 16 * 7)

            def turn_h(i, u):
                k = i * PER + u
                pe.wait_ge(s_h, k + 1)
                wait(pe, s_hT, k)
                for j in range(NT):
                    last = pe.transpose(p_hT[:, j * P:(j + 1) * P], hb[:, u % 2, j], ident[:])
                last.then_inc(s_hTp, 1)

            def linear1(i, u):
                k = i * PER + u
                pe.wait_ge(s_hT, k + 1)
                pe.wait_ge(s_agg, k + 1)
                wait(pe, s_midn, k)
                for j in range(NT):
                    o = p_pre[:, j * F:(j + 1) * F]
                    pe.matmul(o, ones_b[:, :], bias_parts[:, 0:F], start=True, stop=False)
                    pe.matmul(o, hT[:, u % 2, j], w1[:, 0], start=False, stop=True)
                    last = pe.matmul(p_agg[:, j * F:(j + 1) * F], agg[:, u % 2, j], w1[:, 1], start=True, stop=True)
                last.then_inc(s_pre, 1)

            def turn_mid(i, u):
                k = i * PER + u
                pe.wait_ge(s_midn, k + 1)
                wait(pe, s_pn, k)
                for a in range(2):
                    for j in range(NT):
                        last = pe.transpose(p_mT[:, (a * NT + j) * P:(a * NT + j + 1) * P], midn[:, j, a * P:(a + 1) * P], ident[:])
                last.then_inc(s_mT, 1)

            def linear2(i, u):
                k = i * PER + u
                pe.wait_ge(s_act, k + 1)
                wait(pe, s_x1, k)
                for j in range(NT):
                    o = p_out[:, j * P:(j + 1) * P]
                    pe.matmul(o, ones_b[:, :], bias_parts[:, F:F + P], start=True, stop=False)
                    pe.matmul(o, act_t[:, 0, j], w2[:, 0], start=False, stop=False)
                    last = pe.matmul(o, act_t[:, 1, j], w2[:, 1], start=False, stop=True)
                last.then_inc(s_out, 1)

            def node_step(i, u):
                if is_step(i, u, 1):
                    linear1(*before(i, u, 1))
                if is_step(i, u, 0):
                    turn_h(i, u)
                if is_step(i, u, 1):
                    turn_mid(*before(i, u, 1))
                if is_step(i, u, 2):
                    linear2(*before(i, u, 2))
            node_steps(pe, node_step, 2)

            sums(1)
            general_sums(1)

            def turn_sums(i, u):
                k = i * PER + u
                pe.wait_ge(s_agg2, k + 1)
                wait(pe, s_f, k - 1)
                turned = (p_hT, p_mT)[u % 2]
                for j in range(NT):
                    last = pe.transpose(turned[:, j * P:(j + 1) * P], agg[:, u % 2, j], ident[:])
                last.then_inc(s_fT, 1)
            node_steps(pe, turn_sums)

        @block.vector
        def _(dve):
            links = [0]

            def link(ins):
                links[0] += 1
                ins.then_inc(s_chain, 1)
                dve.wait_ge(s_chain, links[0])

            link(dve.memset(raw[:], PAD))
            dve.sem_inc(s_raw_set, 1)
            dve.memset(ones[:], 1.0)
            dve.memset(ones_b[:], 1.0)
            dve.memset(bias_parts[:], 0.0)
            link(dve.memset(eps[:], EPS))
            dve.sem_inc(s_ones, 1)
            dve.memset(cnt[:], 0.0)
            dve.wait_ge(s_pool_const, 3)
            dve.tensor_copy(iota, iota_i[:])
            dve.wait_ge(s_raw, 32)
            link(dve.tensor_copy(rawf[:], raw[:]))
            link(dve.tensor_copy(first[:], rawf[:].rearrange("c (r e) -> c e r", r=R)[:, 0, :]))
            link(dve.memset(raw[:], 0))
            dve.sem_inc(s_raw_set, 1)
            for r in range(R):
                last = dve.tensor_scalar(rawf[:, r * GE:(r + 1) * GE], rawf[:, r * GE:(r + 1) * GE], first[:, r:r + 1], None, ALU.subtract)
            link(last)
            dve.sem_inc(s_rawf, 1)
            link(dve.tensor_scalar(inside, rawf[:], 0.0, None, ALU.is_ge))
            link(dve.scalar_tensor_tensor(out=inside, in0=rawf[:], scalar=float(W), in1=inside, op0=ALU.is_lt, op1=ALU.mult))
            dve.tensor_reduce(good[:], inside, AX_X, ALU.add).then_inc(s_good, 1)

            def take_turned(into):
                for b, bank_ in enumerate((p_hT, p_pre, p_agg, p_mT)):
                    n = min(4, RT - 4 * b)
                    last = dve.tensor_copy(into[:, :, 4 * b:4 * b + n].rearrange("p c t -> p t c"),
                                           bank_[:, :].rearrange("p (t c) -> p t c", c=P)[:, 0:n, 0:NC])
                return last
            dve.wait_ge(s_turned, 1)
            take_turned(local).then_inc(s_local, 1)
            dve.wait_ge(s_good, 2)
            link(dve.tensor_scalar(good[0:1, :], p_out[0:1, 0:1], -1.0, float(E), ALU.mult, ALU.add))
            dve.tensor_scalar(flag[:], good[0:1, :], 1.0, None, ALU.min).then_inc(s_flag, 1)
            dve.wait_ge(s_raw, 64)
            link(dve.tensor_copy(rawf[:], raw[:]))
            dve.sem_inc(s_rawf, 1)
            dve.wait_ge(s_turned, 2)
            take_turned(source).then_inc(s_source, 1)
            dve.wait_ge(s_const, 16 * 7)
            link(dve.tensor_copy(bias_hi[:], bias[:]))
            link(dve.tensor_tensor(bias_rest[:], bias[:], bias_hi[:], ALU.subtract))
            link(dve.tensor_copy(bias_mid[:], bias_rest[:]))
            dve.tensor_copy(bias_parts[0:1, :], bias_hi[0:1, :])
            dve.tensor_copy(bias_parts[32:33, :], bias_mid[32:33, :])
            dve.tensor_tensor(bias_parts[64:65, :], bias_rest[64:65, :], bias_mid[64:65, :], ALU.subtract)
            dve.tensor_scalar(gbn[:], gb[:], -1.0, None, ALU.mult)
            dve.tensor_scalar(slope[:, 1:2], slope[:, 0:1], -1.0, None, ALU.mult).then_inc(s_gbn, 1)

            def sums(layer):
                adds = 4 if layer == 0 else 2

                def one_hot(i, u):
                    c = i * RING + u
                    wait(dve, s_win[layer], c - 1)
                    dve.tensor_tensor(hot[:, u % 2], local[:, bass.ds(c, 1), :].rearrange("p c t -> p (c t)").to_broadcast([P, RT, W]),
                                      iota.rearrange("p (a w) -> p a w", a=1).to_broadcast([P, RT, W]), ALU.is_equal).then_inc(s_hot[layer], 1)

                def add_windows(i, u):
                    c = i * RING + u
                    dve.wait_ge(s_win[layer], c + 1)
                    for r in range(R):
                        node = dve.value_load(first_row[0:1, bass.ds(c * R + r, 1)], min_val=0, max_val=N - 1)
                        wait(dve, s_add[layer], c * adds + r * adds // R)
                        place = acc[:, bass.ds(node, W)]
                        dve.tensor_tensor(place, p_win[u % 2][:, r * W:(r + 1) * W], place, ALU.add).then_inc(s_add[layer], 1)
                        if layer == 0:
                            place = cnt[0:1, bass.ds(node, W)]
                            dve.tensor_tensor(place, p_cnt(u)[:, r * W:(r + 1) * W], place, ALU.add).then_inc(s_add[0], 1)

                def step(i, u):
                    if not isinstance(i, int) or i * RING + u < NC:
                        one_hot(i, u)
                    if not isinstance(i, int) or i * RING + u > 0:
                        add_windows(*before(i, u, 1, RING))
                chunks(dve, step)
                add_windows(*divmod(NC - 1, RING))
                dve.wait_ge(s_add[layer], NC * adds)

            def general_sums(layer):
                with dve.If(general(dve) > 0):
                    dve.memset(acc[:], 0.0)
                    if layer == 0:
                        dve.memset(cnt[:], 0.0)
                    dve.drain().then_inc(s_ga[layer], 1)

                    def slow_tile(n, k):
                        dve.wait_ge(s_gd[layer], 16 * k + 16)
                        dve.wait_ge(s_gt[layer], k + 1)
                        dve.nop(nofuse=True)
                        with dve.Fori(0, n) as e:
                            node = dve.value_load(slow_dst[0:1, bass.ds(e, 1)], min_val=0, max_val=N - 1)
                            place = acc[:, bass.ds(node, 1)]
                            dve.tensor_tensor(place, p_hT[:, bass.ds(e, 1)], place, ALU.add)
                            if layer == 0:
                                one = cnt[0:1, bass.ds(node, 1)]
                                dve.tensor_scalar(one, one, 1.0, None, ALU.add)
                            dve.drain()
                        dve.drain().then_inc(s_ga[layer], 1)
                    with dve.Fori(0, SE) as t:
                        slow_tile(P, t)
                    if SREST:
                        slow_tile(SREST, SE)
                dve.sem_inc(s_final[layer], 1)

            dve.wait_ge(s_first, 32)
            dve.wait_ge(s_acc0, 1)
            sums(0)
            general_sums(0)

            dve.wait_ge(s_cntT, 1)
            dve.tensor_scalar(cnt_any[:], p_agg[:, 0:NTILES], 1.0, None, ALU.min)
            dve.tensor_scalar(cnt1[:], p_agg[:, 0:NTILES], 1.0, None, ALU.max).then_inc(s_cnt1, 1)
            dve.wait_ge(s_cnt1, 1)
            dve.reciprocal(inv_cnt[:], cnt1[:])
            dve.wait_ge(s_csd, 1)
            link(dve.reciprocal(deg_is[:], cnt_sd[:]))
            dve.tensor_tensor(deg_is[:], deg_is[:], cnt_any[:], ALU.mult).then_inc(s_deg, 1)
            dve.wait_ge(s_deg, 1)

            s_lx, s_lm, s_l1 = s_links

            def norm_stats(which, k, s_link, at, tiles, done, taken):
                wait(dve, taken, k)
                for j in range(NT):
                    last = dve.bn_stats(stats[:, which, j], tiles[j])
                last.then_inc(s_link, 1)
                dve.wait_ge(s_link, at)
                dve.nop(nofuse=True)
                for j in range(NT):
                    last = dve.bn_aggr(mv[:, which, j], stats[:, which, j])
                last.then_inc(done, 1)
                dve.wait_ge(done, k + 1)

            def x_stats(i, u):
                k = i * PER + u
                lastk = isinstance(k, int) and k == NK - 1
                dve.wait_ge(s_x[u], i * 16 + (16 * NT if lastk else 16))
                norm_stats(0, k, s_lx, k * 2 + 1, [xin[:, u, j] for j in range(NT)], s_var, s_sd)
                dve.wait_ge(s_sd, k + 1)
                wait(dve, s_h, k)
                dve.reciprocal(rstd[:, 0], sd[:, 0]).then_inc(s_lx, 1)
                dve.wait_ge(s_lx, k * 2 + 2)
                dve.scalar_tensor_tensor(out=nb[:, 0], in0=mv[:, 0, :, 0], scalar=-1.0, in1=rstd[:, 0], op0=ALU.mult, op1=ALU.mult).then_inc(s_nb, 1)

            def mid_norm(i, u):
                k = i * PER + u
                dve.wait_ge(s_pre, k + 1)
                dve.wait_ge(s_prec, k + 1)
                for j in range(NT):
                    last = dve.scalar_tensor_tensor(out=mid[:, j], in0=p_agg[:, j * F:(j + 1) * F], scalar=inv_cnt[:, bass.ds(k * NT + j, 1)],
                                                    in1=pre[:, j], op0=ALU.mult, op1=ALU.add)
                last.then_inc(s_lm, 1)
                dve.wait_ge(s_lm, k * 3 + 1)
                norm_stats(1, k, s_lm, k * 3 + 2, [mid[:, j] for j in range(NT)], s_mid, s_midsd)
                dve.wait_ge(s_midsd, k + 1)
                dve.reciprocal(rstd[:, 1], sd[:, 1]).then_inc(s_lm, 1)
                dve.wait_ge(s_lm, k * 3 + 3)
                wait(dve, s_mT, k)
                for j in range(NT):
                    last = dve.tensor_scalar(midn[:, j], mid[:, j], mv[:, 1, j, 0:1], rstd[:, 1, j:j + 1], ALU.subtract, ALU.mult)
                last.then_inc(s_midn, 1)

            def prelu(i, u):
                k = i * PER + u
                dve.wait_ge(s_pn, k + 1)
                wait(dve, s_out, k)
                dve.scalar_tensor_tensor(out=act_t[:], in0=neg[:], scalar=slope[:, 1:2], in1=pos[:], op0=ALU.mult, op1=ALU.add).then_inc(s_act, 1)

            def x1_stats(i, u):
                k = i * PER + u
                dve.wait_ge(s_out, k + 1)
                i2, u2 = before(i, u, 2)
                wait(dve, s_x1st[u2], i2 * 16 + 16)
                wait(dve, s_h2, k - 1)
                dve.tensor_tensor(x1[:, u % 2], p_out[:, 0:NT * P].rearrange("p (j h) -> p j h", j=NT), xin[:, u], ALU.add).then_inc(s_l1, 1)
                dve.wait_ge(s_l1, k * 4 + 1)
                norm_stats(2, k, s_l1, k * 4 + 2, [x1[:, u % 2, j] for j in range(NT)], s_x1, s_x1sd)
                dve.wait_ge(s_x1sd, k + 1)
                wait(dve, s_h2, k)
                dve.reciprocal(rstd[:, 2], sd[:, 2]).then_inc(s_l1, 1)
                dve.wait_ge(s_l1, k * 4 + 3)
                dve.tensor_tensor(rstd[:, 2], rstd[:, 2], deg_is[:, bass.ds(k * NT, NT)], ALU.mult).then_inc(s_l1, 1)
                dve.wait_ge(s_l1, k * 4 + 4)
                dve.scalar_tensor_tensor(out=nb[:, 2], in0=mv[:, 2, :, 0], scalar=-1.0, in1=rstd[:, 2], op0=ALU.mult, op1=ALU.mult).then_inc(s_x1nb, 1)

            def node_step(i, u):
                if is_step(i, u, 1):
                    mid_norm(*before(i, u, 1))
                if is_step(i, u, 0):
                    x_stats(i, u)
                if is_step(i, u, 2):
                    prelu(*before(i, u, 2))
                    x1_stats(*before(i, u, 2))
            node_steps(dve, node_step, 2)

            dve.wait_ge(s_clear, NK)
            sums(1)
            general_sums(1)

            def result(i, u):
                k = i * PER + u
                dve.wait_ge(s_fT, k + 1)
                dve.wait_ge(s_xl[u], i * 16 + 16)
                i2, u2 = before(i, u, 2)
                wait(dve, s_st[u2], i2 * 16 + 16)
                turned = (p_hT, p_mT)[u % 2]
                for j in range(NT):
                    last = dve.scalar_tensor_tensor(out=x1[:, u % 2, j], in0=turned[:, j * P:(j + 1) * P], scalar=deg_is[:, bass.ds(k * NT + j, 1)],
                                                    in1=xin[:, u, j], op0=ALU.mult, op1=ALU.add)
                last.then_inc(s_f, 1)
            node_steps(dve, result)


_INS = ['x', 'src', 'dst', 'edge_attr_128', 'L0_gnn_W1', 'L0_gnn_b1', 'L0_gnn_gamma', 'L0_gnn_beta', 'L0_gnn_prelu_a', 'L0_gnn_W2', 'L0_gnn_b2']


def kernel(**inputs):
    import numpy as _np
    import concourse.bacc as _bacc
    from concourse import mybir as _mybir
    from concourse.bass_utils import run_bass_kernel_spmd as _run

    nc = _bacc.Bacc("TRN2", target_bir_lowering=False, num_devices=1)
    arrays, args = {}, []
    for name in _INS:
        a = _np.ascontiguousarray(inputs[name])
        arrays[f"in_{name}_dram"] = a
        args.append(nc.dram_tensor(f"in_{name}_dram", a.shape, _mybir.dt.from_np(a.dtype), kind="ExternalInput").ap())
    n, h = inputs['x'].shape
    padded = -(-n // (NT * P)) * NT * P
    args.append(nc.dram_tensor("table", (padded, h), F32, kind="Internal").ap())
    args.append(nc.dram_tensor("x1_dram", (padded, h), F32, kind="Internal").ap())
    args.append(nc.dram_tensor("out_0_dram", (n, h), F32, kind="ExternalOutput").ap())
    gnn_kernel(nc, *args)
    r = _run(nc, [arrays], core_ids=[0])
    return r.results[0]["out_0_dram"]
```

```python
from contextlib import ExitStack

import concourse.bass as bass
from concourse import mybir

F32 = mybir.dt.float32
F32R = mybir.dt.float32r
BF16 = mybir.dt.bfloat16
I32 = mybir.dt.int32
ALU = mybir.AluOpType
ACT = mybir.ActivationFunctionType
AX_X = mybir.AxisListType.X

P = 128
T = 6
R = 3
W = 56
RING = 6
SPLIT = 4
SW = P + 2
NT = 2
POS = 12
STEP_AT = (0, 6)
SUB_DVE = 2
EPS = 1e-5
PAD = -(1 << 20)


def gnn_kernel(nc, x, src, dst, attr, W1, b1, gamma, beta, prelu_a, W2, b2, table, x1_dram, out):
    N, H = x.shape
    E = attr.shape[0]
    F = W1.shape[1]
    assert H == P and F == 2 * P and W1.shape[0] == 2 * P
    GE = T * P
    CE = R * GE
    NC = -(-E // CE)
    NG = -(-E // GE)
    LAST = E - (NC - 1) * CE
    LAST_G = E - (NG - 1) * GE
    LAST_DMAS = (LAST_G >= T) + (LAST_G % T > 0)
    NK = -(-N // (NT * P))
    NTILES = NK * NT
    NPAD = NTILES * P + 64
    TAIL = N - (NTILES - 1) * P
    SE, SREST = E // P, E % P
    assert NC <= P and POS % RING == 0 and POS % SPLIT == 0 and 0 < TAIL <= P and NT == 2

    SAFE = 4
    G_END, G_ALL = NG // POS - 1, -(-(NG + 6) // POS)
    K_END, K_ALL = NK // 2, -(-NK // 2) + 2
    assert G_END > SAFE and K_END > SAFE

    with ExitStack() as ctx:
        def sb(name, shape, dt=F32):
            return ctx.enter_context(nc.sbuf_tensor(name, shape, dt))

        def bank(name):
            return ctx.enter_context(nc.psum_tensor(name, [P, 512], F32))

        def sem(name):
            return ctx.enter_context(nc.semaphore(name))

        acc = sb("acc", [P, NPAD])
        cnt = sb("cnt", [1, NPAD])
        rows = sb("rows", [P, RING, T, P])
        split = sb("split", [P, SPLIT, 2, T, SW], F32R)
        hot = sb("hot", [P, SPLIT, T, W], F32R)
        local = sb("local", [P, NC * R, T])
        source = sb("source", [P, NC * R, T], I32)
        fw = sb("fw", [W, 2, SW])
        first = sb("first", [P, R])
        first_row = sb("first_row", [1, NG], I32)
        good = sb("good", [P, 1])
        flag = sb("flag", [1, 1], I32)
        index = sb("index", [P, RING, T], I32)
        ident = sb("ident", [P, P])
        iota_i = sb("iota_i", [P, W], I32)
        iota = sb("iota", [P, W])
        ones = sb("ones", [P, 1])
        ones_b = sb("ones_b", [P, P], BF16)
        zeros = sb("zeros", [P, NT * P])
        eps = sb("eps", [P, 1])
        w1 = sb("w1", [P, 2, F])
        w2 = sb("w2", [P, 2, P])
        bias = sb("bias", [P, F + P])
        bias_hi = sb("bias_hi", [P, F + P], BF16)
        bias_mid = sb("bias_mid", [P, F + P], BF16)
        bias_parts = sb("bias_parts", [P, F + P], BF16)
        gb = sb("gb", [P, 2, 2])
        gbn = sb("gbn", [P, 2, 2])
        slope = sb("slope", [P, 2])
        deg_is = sb("deg_is", [P, NTILES])
        stats = sb("stats", [P, 3, NT, 6])
        mv = sb("mv", [P, 3, NT, 2])
        sd = sb("sd", [P, 3, NT])
        rstd = sb("rstd", [P, 3, NT])
        nb = sb("nb", [P, 3, NT])
        cnt1 = sb("cnt1", [P, NT])
        cnt_any = sb("cnt_any", [P, NT])
        inv_cnt = sb("inv_cnt", [P, NT])
        cnt_sd = sb("cnt_sd", [P, NT])
        inv_sd = sb("inv_sd", [P, NT])
        cnt_row = sb("cnt_row", [1, NT * P])
        hTc = sb("hTc", [P, NT * P + NT])
        x1 = sb("x1", [P, 2, NT, P])
        h2 = sb("h2", [P, 2, NT, P])
        slow_dst = sb("slow_dst", [1, P], I32)
        slow_src = sb("slow_src", [P, 1], I32)

        work = sb("work", [P, 38 * P])
        raw = work[:, 0:CE].bitcast(I32)
        rawf = work[:, CE:2 * CE]
        inside = rows[:].rearrange("p a t h -> p (a t h)")[:, (RING - R) * GE:RING * GE]

        def part(at, a, b):
            return work[:, at * P:at * P + a * b].rearrange("p (a b) -> p a b", a=a)

        xa = [part(NT * u, NT, P) for u in range(2)]
        xb = [part(4 + NT * u, NT, P) for u in range(2)]
        agg = [part(8 + NT * u, NT, P) for u in range(2)]
        hb = part(12, NT, P)
        pre = part(14, NT, F)
        mid = part(18, NT, F)
        midn = part(22, NT, F)
        pos = part(26, 2 * NT, P)
        neg = part(30, 2 * NT, P)
        act_t = part(34, 2 * NT, P)

        p_sum = [bank(f"p_sum{i}") for i in range(2)]
        p_win = bank("p_win")
        p_hT = bank("p_hT")
        p_pre = bank("p_pre")
        p_agg = bank("p_agg")
        p_mT = bank("p_mT")
        p_out = bank("p_out")

        s_fill = sem("raw_filled")
        s_raw = sem("raw_in")
        s_first = sem("first_row_in")
        s_const = sem("weights_in")
        s_ident = sem("ident_ready")
        s_iota = sem("iota_ready")
        s_ones = sem("ones_ready")
        s_gbn = sem("bias_parts_ready")
        s_rawf = sem("raw_as_float")
        s_turned = sem("raw_turned")
        s_local = sem("local_ready")
        s_source = sem("source_ready")
        s_good = sem("good_summed")
        s_flag = sem("flag_ready")
        s_acc0 = sem("acc_zeroed")
        s_chain = sem("dve_start_chain")
        s_rows = [[sem(f"rows{l}_in{i}") for i in range(RING)] for l in range(2)]
        s_hot = [sem(f"hot{l}_ready") for l in range(2)]
        s_win = [sem(f"window{l}_ready") for l in range(2)]
        s_add = [sem(f"window{l}_added") for l in range(2)]
        s_final = [sem(f"sums{l}_final") for l in range(2)]
        s_hi = sem("upper_ready")
        s_lo_d = sem("lower_ready_dve")
        s_lo_p = sem("lower_ready_pool")
        s_sum = sem("group_summed")
        s_fw = sem("group_copied")
        s_index = sem("index_ready")
        s_xl = [sem(f"x1_in{u}") for u in range(2)]
        s_agg2 = sem("agg2_copied")
        s_fT = sem("sums_turned")
        s_f = sem("result_ready")
        s_st = [sem(f"result_stored{u}") for u in range(2)]
        s_gd = [sem(f"general{l}_dst_in") for l in range(2)]
        s_gi = sem("general_src_in")
        s_gr = [sem(f"general{l}_rows_in") for l in range(2)]
        s_gt = [sem(f"general{l}_turned") for l in range(2)]
        s_ga = [sem(f"general{l}_added") for l in range(2)]

        STEP_SEMS = ("agg clear stat0 var sd rstd0 nb h hTp hT pre prec any cnt midc stat1 midv msd rstd1 midn mT pn act "
                     "out x1c stat2 x1v x1sd rstd2 scale2 x1nb h2").split()

        def step_sems(tag):
            S = {name: sem(f"{tag}_{name}") for name in STEP_SEMS}
            for name in ("xa_in", "xb_in", "x1_stored", "h2_stored"):
                S[name] = [sem(f"{tag}_{name}{u}") for u in range(2)]
            return S

        block = ctx.enter_context(nc.Block())

        def wait(eng, s, value):
            if not isinstance(value, int) or value > 0:
                eng.wait_ge(s, value)

        def turns(eng, turn, safe, end, total):
            for i in range(safe):
                turn(i)
            with eng.Fori(safe, end) as i:
                turn(i)
            for i in range(end, total):
                turn(i)

        def run(eng, group_ops, step_ops, S):
            def turn(i):
                for p in range(POS):
                    for lag, f in sorted(group_ops, key=lambda o: -o[0]):
                        gi, gp = i + (p - lag) // POS, (p - lag) % POS
                        if not isinstance(gi, int) or 0 <= gi * POS + gp < NG:
                            f(gi, gp)
                    for lag, f in sorted(step_ops, key=lambda o: -o[0]):
                        for s in range(2):
                            back, rest = divmod(p - STEP_AT[s] - lag, POS)
                            ki = i + back
                            if rest == 0 and (not isinstance(ki, int) or 0 <= 2 * ki + s < NK):
                                f(S, ki, s)
            if min([lag for lag, f in group_ops + step_ops]) < 0:
                turn(-1)
            if group_ops:
                turns(eng, turn, SAFE, G_END, G_ALL)
            else:
                turns(eng, turn, SAFE, K_END, K_ALL)

        def last_slots(s_list, i_total=NK):
            return [(s_list[u], (i_total - u + 1) // 2) for u in range(2)]

        def general(eng):
            eng.wait_ge(s_flag, 1)
            return eng.value_load(flag[0:1, 0:1], min_val=0, max_val=1)

        def node_rows(dram, k):
            return dram[bass.ds(k * (NT * P), NT * P)].rearrange("(j p) h -> p j h", p=P)

        S1 = step_sems("n")

        @block.sync
        def _(sp):
            body = (NC - 1) * CE
            for n, edges in enumerate((dst, src)):
                sp.wait_ge(s_fill, n + 1)
                sp.dma_start(raw[0:NC - 1, :], edges[0:body].rearrange("(c e) -> c e", e=CE)).then_inc(s_raw, 16)
                sp.dma_start(raw[NC - 1:NC, 0:LAST], edges[body:E].rearrange("(c e) -> c e", c=1)).then_inc(s_raw, 16)
                if n == 0:
                    with nc.allow_non_contiguous_dma(reason="one value of each group"):
                        whole = GE * (NG - 1)
                        sp.dma_start(first_row[0:1, 0:NG - 1], dst[0:whole].rearrange("(g e) -> e g", e=GE)[0:1, :]).then_inc(s_first, 16)
                        sp.dma_start(first_row[0:1, NG - 1:NG], dst[whole:whole + 1].rearrange("(g e) -> e g", e=1)).then_inc(s_first, 16)

            def load_rows(i, p):
                g, slot = i * POS + p, p % RING
                if isinstance(g, int) and g == RING - R:
                    sp.wait_ge(s_good, 1)
                wait(sp, s_lo_d, g - RING + 1)
                wait(sp, s_lo_p, g - RING + 1)
                if isinstance(g, int) and g == NG - 1:
                    e, full = g * GE, LAST_G // T
                    if full:
                        sp.dma_start(rows[0:full, slot].rearrange("p t h -> p (t h)"),
                                     attr[e:e + full * T].rearrange("(p t) h -> p (t h)", t=T)).then_inc(s_rows[0][slot], 16)
                    if LAST_G % T:
                        sp.dma_start(rows[full:full + 1, slot, 0:LAST_G % T].rearrange("p t h -> p (t h)"),
                                     attr[e + full * T:E].rearrange("(p t) h -> p (t h)", p=1)).then_inc(s_rows[0][slot], 16)
                else:
                    sp.dma_start(rows[:, slot].rearrange("p t h -> p (t h)"),
                                 attr[bass.ds(g * GE, GE)].rearrange("(p t) h -> p (t h)", t=T)).then_inc(s_rows[0][slot], 16)

            def load_x(into, landed, freed):
                def f(S, i, s):
                    k = 2 * i + s
                    wait(sp, S[freed], k - 1)
                    if isinstance(k, int) and k == NK - 1:
                        for j in range(NT):
                            n, m = (k * NT + j) * P, P if j < NT - 1 else TAIL
                            sp.dma_start(into[s][0:m, j], x[n:n + m]).then_inc(S[landed][s], 16)
                    else:
                        sp.dma_start(into[s], node_rows(x, k)).then_inc(S[landed][s], 16)
                return f

            def store_nodes(S, i, s):
                k = 2 * i + s
                sp.wait_ge(S["h2"], k + 1)
                sp.dma_start(node_rows(table, k), h2[:, s]).then_inc(S["h2_stored"][s], 16)
                sp.dma_start(node_rows(x1_dram, k), x1[:, s]).then_inc(S["x1_stored"][s], 16)

            step_ops = [(0, load_x(xa, "xa_in", "h")), (12, load_x(xb, "xb_in", "x1c")), (22, store_nodes)]
            run(sp, [(-4, load_rows)], [], None)

            def slow_tiles(layer):
                def slow_tile(t, n):
                    sp.wait_ge(s_ga[layer], t + 1)
                    sp.dma_start(slow_dst[0:1, 0:n], dst[bass.ds(t * P, n)].rearrange("(a e) -> a e", a=1)).then_inc(s_gd[layer], 16)
                    if layer == 0:
                        sp.dma_start(rows[0:n, 0, 0, :], attr[bass.ds(t * P, n)]).then_inc(s_gr[0], 16)
                    else:
                        sp.dma_start(slow_src[0:n, :], src[bass.ds(t * P, n)].rearrange("(e a) -> e a", a=1)).then_inc(s_gi, 16)
                with sp.Fori(0, SE) as t:
                    slow_tile(t, P)
                if SREST:
                    slow_tile(SE, SREST)

            with sp.If(general(sp) > 0):
                slow_tiles(0)
            sp.wait_ge(s_source, 1)
            run(sp, [], step_ops, S1)
            with sp.If(general(sp) > 0):
                slow_tiles(1)

            for s, n in last_slots(S1["x1_stored"]):
                sp.wait_ge(s, 16 * n)

            def load_x1(i, s):
                k = 2 * i + s
                wait(sp, s_f, k - 1)
                sp.dma_start(xb[s], node_rows(x1_dram, k)).then_inc(s_xl[s], 16)

            def store_out(i, s):
                k = 2 * i + s
                sp.wait_ge(s_f, k + 1)
                if isinstance(k, int) and k == NK - 1:
                    for j in range(NT):
                        n, m = (k * NT + j) * P, P if j < NT - 1 else TAIL
                        sp.dma_start(out[n:n + m], x1[0:m, s, j]).then_inc(s_st[s], 16)
                else:
                    sp.dma_start(node_rows(out, k), x1[:, s]).then_inc(s_st[s], 16)

            def result_turn(i):
                for s in range(2):
                    if not isinstance(i, int) or 2 * i + s < NK:
                        load_x1(i, s)
                    if not isinstance(i, int) or 0 <= 2 * i + s - 1 < NK:
                        store_out(i + (s - 1) // 2, (s - 1) % 2)
            turns(sp, result_turn, 2, K_END, K_ALL)
            for u, (s, n) in enumerate(last_slots(s_st)):
                sp.wait_ge(s, 16 * (n + (NT - 1 if u == (NK - 1) % 2 else 0)))

        @block.gpsimd
        def _(pool):
            pool.memset(ident[:], 0.0).then_inc(s_ident, 1)
            pool.wait_ge(s_ident, 1)
            pool.affine_select(out=ident[:], in_=ident[:], compare_op=ALU.not_equal, fill=1.0, base=0,
                               pattern=[[-1, P]], channel_multiplier=1).then_inc(s_ident, 1)
            pool.iota(iota_i[:], pattern=[[1, W]], base=0, channel_multiplier=0).then_inc(s_iota, 1)
            pool.memset(zeros[:], 0.0)
            pool.memset(acc[:], 0.0).then_inc(s_acc0, 1)

            def lower(i, p):
                g = i * POS + p
                pool.wait_ge(s_hi, g + 1)
                pool.tensor_tensor(split[:, p % SPLIT, 1, SUB_DVE:T, 0:P], rows[:, p % RING, SUB_DVE:T],
                                   split[:, p % SPLIT, 0, SUB_DVE:T, 0:P].bitcast(F32), ALU.subtract).then_inc(s_lo_p, 1)

            def move_agg(S, i, s):
                k = 2 * i + s
                wait(pool, S["pre"], k - 1)
                wait(pool, S["hTp"], k)
                nodes = acc[:, bass.ds(k * (NT * P), NT * P)]
                pool.tensor_copy(agg[s].rearrange("p j h -> p (j h)"), nodes)
                pool.tensor_copy(cnt_row[:], cnt[0:1, bass.ds(k * (NT * P), NT * P)]).then_inc(S["agg"], 1)
                pool.wait_ge(S["agg"], k + 1)
                pool.nop(nofuse=True)
                pool.tensor_copy(nodes, zeros[:]).then_inc(S["clear"], 1)

            run(pool, [(1, lower)], [], None)
            pool.wait_ge(s_final[0], 1)
            pool.wait_ge(s_source, 1)
            run(pool, [], [(6, move_agg)], S1)

            for s, n in last_slots(S1["h2_stored"]):
                pool.wait_ge(s, 16 * n)

            def gather(i, p):
                g, slot = i * POS + p, p % RING
                pool.wait_ge(s_index, g + 1)
                wait(pool, s_win[1], g - RING + 1)
                pool.nop(nofuse=True)
                for t in range(T):
                    pool.indirect_dma_start(rows[:, slot, t], None, table,
                                            bass.IndirectOffsetOnAxis(ap=index[:, slot, t:t + 1], axis=0)).then_inc(s_rows[1][slot], 16)
            run(pool, [(0, gather)], [], None)

            with pool.If(general(pool) > 0):
                def slow_tile(t, n):
                    pool.wait_ge(s_gi, 16 * t + 16)
                    pool.nop(nofuse=True)
                    pool.indirect_dma_start(rows[0:n, 0, 0, :], None, table,
                                            bass.IndirectOffsetOnAxis(ap=slow_src[0:n, 0:1], axis=0)).then_inc(s_gr[1], 16)
                with pool.Fori(0, SE) as t:
                    slow_tile(t, P)
                if SREST:
                    slow_tile(SE, SREST)

        @block.scalar
        def _(act):
            act.dma_start(w1[:], W1.rearrange("(a p) f -> p a f", p=P)).then_inc(s_const, 16)
            act.dma_start(w2[:], W2.rearrange("(a p) h -> p a h", p=P)).then_inc(s_const, 16)
            act.dma_start(bias[:, 0:F], b1.rearrange("(a f) -> a f", a=1).to_broadcast([P, F])).then_inc(s_const, 16)
            act.dma_start(bias[:, F:F + P], b2.rearrange("(a f) -> a f", a=1).to_broadcast([P, P])).then_inc(s_const, 16)
            with nc.allow_non_contiguous_dma(reason="512 single values"):
                act.dma_start(gb[:, 0, :], gamma.rearrange("(a p) -> p a", p=P)).then_inc(s_const, 16)
                act.dma_start(gb[:, 1, :], beta.rearrange("(a p) -> p a", p=P)).then_inc(s_const, 16)
            act.dma_start(slope[:, 0:1], prelu_a.rearrange("(a f) -> a f", a=1).to_broadcast([P, 1])).then_inc(s_const, 16)

            def upper(i, p):
                g = i * POS + p
                act.wait_ge(s_rows[0][p % RING], (i * (POS // RING) + p // RING) * 16 + (16 * LAST_DMAS if isinstance(g, int) and g == NG - 1 else 16))
                wait(act, s_sum, g - SPLIT + 1)
                act.copy(split[:, p % SPLIT, 0, :, 0:P], rows[:, p % RING]).then_inc(s_hi, 1)

            def copy_sums(i, p):
                g = i * POS + p
                act.wait_ge(s_sum, g + 1)
                wait(act, s_win[0], g - 1)
                act.copy(fw[:, p % 2], p_sum[p % 2][0:W, 0:SW]).then_inc(s_fw, 1)

            def x_sd(S, i, s):
                k = 2 * i + s
                act.wait_ge(S["var"], k + 1)
                wait(act, S["rstd0"], k)
                act.activation(sd[:, 0], mv[:, 0, :, 1], ACT.Sqrt, bias=eps[:, 0:1]).then_inc(S["sd"], 1)

            def norm_x(S, i, s):
                k = 2 * i + s
                act.wait_ge(S["nb"], k + 1)
                wait(act, S["hTp"], k)
                for j in range(NT):
                    last = act.activation(hb[:, j], xa[s][:, j], ACT.Relu, scale=rstd[:, 0, j:j + 1], bias=nb[:, 0, j:j + 1])
                last.then_inc(S["h"], 1)

            def copy_hT(S, i, s):
                k = 2 * i + s
                act.wait_ge(S["hTp"], k + 1)
                wait(act, S["pre"], k)
                wait(act, S["any"], k)
                act.copy(hTc[:], p_hT[:, 0:NT * P + NT]).then_inc(S["hT"], 1)

            def copy_pre(S, i, s):
                k = 2 * i + s
                act.wait_ge(S["pre"], k + 1)
                wait(act, S["midc"], k)
                act.copy(pre, p_pre[:, :].rearrange("p (j f) -> p j f", j=NT)).then_inc(S["prec"], 1)

            def mid_sd(S, i, s):
                k = 2 * i + s
                act.wait_ge(S["midv"], k + 1)
                wait(act, S["midn"], k)
                act.activation(cnt_sd[:], cnt1[:], ACT.Sqrt)
                act.activation(sd[:, 1], mv[:, 1, :, 1], ACT.Sqrt, bias=eps[:, 0:1]).then_inc(S["msd"], 1)

            def relus(S, i, s):
                k = 2 * i + s
                act.wait_ge(S["mT"], k + 1)
                wait(act, S["act"], k)
                for a in range(2):
                    t = p_mT[:, a * NT * P:(a + 1) * NT * P].rearrange("p (j h) -> p j h", j=NT)
                    act.activation(pos[:, a * NT:(a + 1) * NT], t, ACT.Relu, scale=gb[:, 0, a:a + 1], bias=gb[:, 1, a:a + 1])
                    last = act.activation(neg[:, a * NT:(a + 1) * NT], t, ACT.Relu, scale=gbn[:, 0, a:a + 1], bias=gbn[:, 1, a:a + 1])
                last.then_inc(S["pn"], 1)

            def x1_sd(S, i, s):
                k = 2 * i + s
                act.wait_ge(S["x1v"], k + 1)
                wait(act, S["rstd2"], k)
                act.activation(sd[:, 2], mv[:, 2, :, 1], ACT.Sqrt, bias=eps[:, 0:1]).then_inc(S["x1sd"], 1)

            def norm_x1(S, i, s):
                k = 2 * i + s
                act.wait_ge(S["x1nb"], k + 1)
                wait(act, S["h2_stored"][s], i * 16)
                for j in range(NT):
                    last = act.activation(h2[:, s, j], x1[:, s, j], ACT.Relu, scale=rstd[:, 2, j:j + 1], bias=nb[:, 2, j:j + 1])
                last.then_inc(S["h2"], 1)

            step_ops = [(4, x_sd), (6, norm_x), (8, copy_hT), (10, copy_pre), (12, mid_sd), (15, relus), (19, x1_sd), (21, norm_x1)]
            run(act, [(0, upper), (3, copy_sums)], [], None)
            act.wait_ge(s_ones, 1)
            act.wait_ge(s_gbn, 1)
            run(act, [], step_ops, S1)

            act.wait_ge(s_source, 1)

            def copy_index(i, p):
                slot = p % RING
                wait(act, s_rows[1][slot], (i * (POS // RING) + p // RING) * (16 * T))
                act.copy(index[:, slot], source[:, bass.ds(i * POS + p, 1), :].rearrange("p g t -> p (g t)")).then_inc(s_index, 1)
            run(act, [(0, copy_index)], [], None)

            act.wait_ge(s_final[1], 1)

            def move_turn(i):
                for s in range(2):
                    if not isinstance(i, int) or 2 * i + s < NK:
                        k = 2 * i + s
                        wait(act, s_fT, k - 1)
                        act.copy(agg[s].rearrange("p j h -> p (j h)"), acc[:, bass.ds(k * (NT * P), NT * P)]).then_inc(s_agg2, 1)
            turns(act, move_turn, 2, K_END, K_ALL)

        @block.tensor
        def _(pe):
            banks = [p_hT, p_pre, p_agg, p_mT, p_out]

            def turn_raw():
                for rt in range(R * T):
                    r, t = rt // T, rt % T
                    v = rawf[0:NC, r * GE:(r + 1) * GE].rearrange("c (p t) -> c t p", t=T)[:, t, :]
                    last = pe.transpose(banks[rt // 4][:, (rt % 4) * P:(rt % 4) * P + NC], v, ident[0:NC, 0:NC])
                last.then_inc(s_turned, 1)

            pe.wait_ge(s_ident, 2)
            pe.wait_ge(s_rawf, 1)
            turn_raw()
            pe.wait_ge(s_good, 1)
            pe.matmul(p_win[0:1, 0:1], good[0:NC, 0:1], ones[0:NC, 0:1], start=True, stop=True).then_inc(s_good, 1)
            pe.wait_ge(s_rawf, 2)
            pe.wait_ge(s_local, 1)
            turn_raw()
            pe.wait_ge(s_flag, 1)
            pe.wait_ge(s_ones, 2)

            def sums(i, p):
                g = i * POS + p
                pe.wait_ge(s_hot[0], g + 1)
                pe.wait_ge(s_hi, g + 1)
                pe.wait_ge(s_lo_d, g + 1)
                pe.wait_ge(s_lo_p, g + 1)
                wait(pe, s_fw, g - 1)
                for t in range(T):
                    for h in range(2):
                        last = pe.matmul(p_sum[p % 2][0:W, 0:SW], hot[:, p % SPLIT, t], split[:, p % SPLIT, h, t],
                                         start=(t == 0 and h == 0), stop=(t == T - 1 and h == 1))
                last.then_inc(s_sum, 1)

            def turn_window(i, p):
                g = i * POS + p
                pe.wait_ge(s_fw, g + 1)
                wait(pe, s_add[0], 2 * g)
                pe.nop(nofuse=True)
                pe.transpose(p_win[:, 0:W], fw[:, p % 2, 0:P], ident[0:W, 0:W])
                pe.transpose(p_win[0:2, 64:64 + W], fw[:, p % 2, P:SW], ident[0:W, 0:W]).then_inc(s_win[0], 1)

            def turn_h(S, i, s):
                k = 2 * i + s
                pe.wait_ge(S["h"], k + 1)
                pe.wait_ge(S["agg"], k + 1)
                wait(pe, S["hT"], k)
                for j in range(NT):
                    pe.transpose(p_hT[:, j * P:(j + 1) * P], hb[:, j], ident[:])
                for j in range(NT):
                    last = pe.matmul(p_hT[:, NT * P + j:NT * P + j + 1], cnt_row[0:1, j * P:(j + 1) * P], ones[0:1, 0:1], start=True, stop=True)
                last.then_inc(S["hTp"], 1)

            def linear1(S, i, s):
                k = 2 * i + s
                pe.wait_ge(S["hT"], k + 1)
                wait(pe, S["prec"], k)
                wait(pe, S["midc"], k)
                for j in range(NT):
                    o = p_pre[:, j * F:(j + 1) * F]
                    pe.matmul(o, ones_b[:, :], bias_parts[:, 0:F], start=True, stop=False)
                    pe.matmul(o, hTc[:, j * P:(j + 1) * P], w1[:, 0], start=False, stop=True)
                    last = pe.matmul(p_agg[:, j * F:(j + 1) * F], agg[s][:, j], w1[:, 1], start=True, stop=True)
                last.then_inc(S["pre"], 1)

            def turn_mid(S, i, s):
                k = 2 * i + s
                pe.wait_ge(S["midn"], k + 1)
                wait(pe, S["pn"], k)
                for a in range(2):
                    for j in range(NT):
                        last = pe.transpose(p_mT[:, (a * NT + j) * P:(a * NT + j + 1) * P], midn[:, j, a * P:(a + 1) * P], ident[:])
                last.then_inc(S["mT"], 1)

            def linear2(S, i, s):
                k = 2 * i + s
                pe.wait_ge(S["act"], k + 1)
                wait(pe, S["x1c"], k)
                for j in range(NT):
                    o = p_out[:, j * P:(j + 1) * P]
                    pe.matmul(o, ones_b[:, :], bias_parts[:, F:F + P], start=True, stop=False)
                    pe.matmul(o, act_t[:, j], w2[:, 0], start=False, stop=False)
                    last = pe.matmul(o, act_t[:, NT + j], w2[:, 1], start=False, stop=True)
                last.then_inc(S["out"], 1)

            step_ops = [(7, turn_h), (9, linear1), (14, turn_mid), (17, linear2)]

            def general_sums(layer):
                with pe.If(general(pe) > 0):
                    def slow_tile(t, n):
                        pe.wait_ge(s_gr[layer], 16 * t + 16)
                        pe.wait_ge(s_ga[layer], t + 1)
                        pe.transpose(p_win[:, 0:n], rows[0:n, 0, 0, :], ident[0:n, 0:n]).then_inc(s_gt[layer], 1)
                    with pe.Fori(0, SE) as t:
                        slow_tile(t, P)
                    if SREST:
                        slow_tile(SE, SREST)

            run(pe, [(2, sums), (4, turn_window)], [], None)
            general_sums(0)
            pe.wait_ge(s_gbn, 1)
            pe.wait_ge(s_const, 16 * 7)
            run(pe, [], step_ops, S1)

            def gathered_sums(i, p):
                g = i * POS + p
                pe.wait_ge(s_hot[1], g + 1)
                pe.wait_ge(s_rows[1][p % RING], (i * (POS // RING) + p // RING) * (16 * T) + 16 * T)
                wait(pe, s_add[1], g - 1)
                for t in range(T):
                    last = pe.matmul(p_sum[p % 2][:, 0:W], rows[:, p % RING, t], hot[:, p % SPLIT, t].bitcast(F32), start=(t == 0), stop=(t == T - 1))
                last.then_inc(s_win[1], 1)
            run(pe, [(0, gathered_sums)], [], None)
            general_sums(1)

            def turn_sums(i):
                for s in range(2):
                    if not isinstance(i, int) or 2 * i + s < NK:
                        k = 2 * i + s
                        pe.wait_ge(s_agg2, k + 1)
                        wait(pe, s_f, k - 1)
                        for j in range(NT):
                            last = pe.transpose((p_hT, p_mT)[s][:, j * P:(j + 1) * P], agg[s][:, j], ident[:])
                        last.then_inc(s_fT, 1)
            turns(pe, turn_sums, 2, K_END, K_ALL)

        @block.vector
        def _(dve):
            links = [0]

            def link(ins):
                links[0] += 1
                ins.then_inc(s_chain, 1)
                dve.wait_ge(s_chain, links[0])

            dve.memset(raw, PAD).then_inc(s_fill, 1)
            dve.memset(ones[:], 1.0)
            dve.memset(ones_b[:], 1.0)
            dve.memset(bias_parts[:], 0.0)
            dve.memset(eps[:], EPS).then_inc(s_ones, 1)
            dve.memset(cnt[:], 0.0)
            dve.wait_ge(s_iota, 1)
            dve.tensor_copy(iota[:], iota_i[:])
            dve.wait_ge(s_raw, 32)
            link(dve.tensor_copy(rawf, raw))
            dve.tensor_scalar(first[:], rawf.rearrange("c (r e) -> c e r", r=R)[:, 0, :], 0.0, None, ALU.max)
            link(dve.memset(raw, 0))
            dve.sem_inc(s_fill, 1)
            for r in range(R):
                last = dve.tensor_scalar(rawf[:, r * GE:(r + 1) * GE], rawf[:, r * GE:(r + 1) * GE], first[:, r:r + 1], None, ALU.subtract)
            link(last)
            dve.sem_inc(s_rawf, 1)
            link(dve.tensor_scalar(inside, rawf, 0.0, None, ALU.is_ge))
            link(dve.scalar_tensor_tensor(out=inside, in0=rawf, scalar=float(W), in1=inside, op0=ALU.is_lt, op1=ALU.mult))
            dve.tensor_reduce(good[:], inside, AX_X, ALU.add).then_inc(s_good, 1)

            def take_turned(into):
                v = into[:].rearrange("p (c r) t -> p c (r t)", r=R)
                for b, bank_ in enumerate((p_hT, p_pre, p_agg, p_mT, p_out)):
                    n = min(4, R * T - 4 * b)
                    last = dve.tensor_copy(v[:, :, 4 * b:4 * b + n].rearrange("p c t -> p t c"),
                                           bank_[:, :].rearrange("p (t c) -> p t c", c=P)[:, 0:n, 0:NC])
                return last
            dve.wait_ge(s_turned, 1)
            take_turned(local).then_inc(s_local, 1)
            dve.wait_ge(s_good, 2)
            for h in range(2):
                v = split[:].bitcast(F32)[:, :, h, :, P:SW]
                last = dve.memset(v, 0.0)
            link(last)
            for b in range(SPLIT):
                last = dve.memset(split[:].bitcast(F32)[:, b, 0, :, P:P + 1], 1.0)
            last.then_inc(s_ones, 1)
            link(dve.tensor_scalar(good[0:1, :], p_win[0:1, 0:1], -1.0, float(E), ALU.mult, ALU.add))
            dve.tensor_scalar(flag[:], good[0:1, :], 1.0, None, ALU.min).then_inc(s_flag, 1)
            dve.wait_ge(s_raw, 64)
            link(dve.tensor_copy(rawf, raw))
            dve.sem_inc(s_rawf, 1)
            dve.wait_ge(s_turned, 2)
            take_turned(source).then_inc(s_source, 1)
            dve.wait_ge(s_const, 16 * 7)
            link(dve.tensor_copy(bias_hi[:], bias[:]))
            link(dve.tensor_tensor(bias[:], bias[:], bias_hi[:], ALU.subtract))
            link(dve.tensor_copy(bias_mid[:], bias[:]))
            dve.tensor_copy(bias_parts[0:1, :], bias_hi[0:1, :])
            dve.tensor_copy(bias_parts[32:33, :], bias_mid[32:33, :])
            dve.tensor_tensor(bias_parts[64:65, :], bias[64:65, :], bias_mid[64:65, :], ALU.subtract)
            dve.tensor_scalar(gbn[:], gb[:], -1.0, None, ALU.mult)
            dve.tensor_scalar(slope[:, 1:2], slope[:, 0:1], -1.0, None, ALU.mult).then_inc(s_gbn, 1)

            def one_hot(layer):
                used = s_sum if layer == 0 else s_win[1]

                def f(i, p):
                    g = i * POS + p
                    wait(dve, used, g - SPLIT + 1)
                    dve.tensor_tensor(hot[:, p % SPLIT], local[:, bass.ds(g, 1), :].rearrange("p g t -> p (g t)").to_broadcast([P, T, W]),
                                      iota[:].rearrange("p (a w) -> p a w", a=1).to_broadcast([P, T, W]), ALU.is_equal).then_inc(s_hot[layer], 1)
                return f

            def lower(i, p):
                g = i * POS + p
                dve.wait_ge(s_hi, g + 1)
                dve.tensor_tensor(split[:, p % SPLIT, 1, 0:SUB_DVE, 0:P], rows[:, p % RING, 0:SUB_DVE],
                                  split[:, p % SPLIT, 0, 0:SUB_DVE, 0:P].bitcast(F32), ALU.subtract).then_inc(s_lo_d, 1)

            def add_window(layer):
                adds = 2 if layer == 0 else 1

                def f(i, p):
                    g = i * POS + p
                    node = dve.value_load(first_row[0:1, bass.ds(g, 1)], min_val=0, max_val=N - 1)
                    dve.wait_ge(s_win[layer], g + 1)
                    wait(dve, s_add[layer], g * adds)
                    place = acc[:, bass.ds(node, W)]
                    window = p_win if layer == 0 else p_sum[p % 2]
                    dve.tensor_tensor(place, window[:, 0:W], place, ALU.add).then_inc(s_add[layer], 1)
                    if layer == 0:
                        place = cnt[0:1, bass.ds(node, W)]
                        dve.tensor_tensor(place, p_win[0:1, 64:64 + W], place, ALU.add).then_inc(s_add[0], 1)
                return f

            def general_sums(layer):
                dve.wait_ge(s_add[layer], NG * (2 if layer == 0 else 1))
                with dve.If(general(dve) > 0):
                    dve.memset(acc[:], 0.0)
                    if layer == 0:
                        dve.memset(cnt[:], 0.0)
                    dve.drain().then_inc(s_ga[layer], 1)

                    def slow_tile(t, n):
                        dve.wait_ge(s_gd[layer], 16 * t + 16)
                        dve.wait_ge(s_gt[layer], t + 1)
                        dve.nop(nofuse=True)
                        with dve.Fori(0, n) as e:
                            node = dve.value_load(slow_dst[0:1, bass.ds(e, 1)], min_val=0, max_val=N - 1)
                            place = acc[:, bass.ds(node, 1)]
                            dve.tensor_tensor(place, p_win[:, bass.ds(e, 1)], place, ALU.add)
                            if layer == 0:
                                one = cnt[0:1, bass.ds(node, 1)]
                                dve.tensor_scalar(one, one, 1.0, None, ALU.add)
                            dve.drain()
                        dve.drain().then_inc(s_ga[layer], 1)
                    with dve.Fori(0, SE) as t:
                        slow_tile(t, P)
                    if SREST:
                        slow_tile(SE, SREST)
                dve.sem_inc(s_final[layer], 1)

            def norm_stats(S, k, which, tiles, stat, done):
                for j in range(NT):
                    last = dve.bn_stats(stats[:, which, j], tiles[j])
                last.then_inc(S[stat], 1)
                dve.wait_ge(S[stat], k + 1)
                dve.nop(nofuse=True)
                for j in range(NT):
                    last = dve.bn_aggr(mv[:, which, j], stats[:, which, j])
                last.then_inc(S[done], 1)

            def x_stats(S, i, s):
                k = 2 * i + s
                dve.wait_ge(S["xa_in"][s], i * 16 + (16 * NT if isinstance(k, int) and k == NK - 1 else 16))
                wait(dve, S["sd"], k)
                wait(dve, S["nb"], k)
                norm_stats(S, k, 0, [xa[s][:, j] for j in range(NT)], "stat0", "var")

            def x_scale(S, i, s):
                k = 2 * i + s
                dve.wait_ge(S["sd"], k + 1)
                wait(dve, S["h"], k)
                dve.reciprocal(rstd[:, 0], sd[:, 0]).then_inc(S["rstd0"], 1)
                dve.wait_ge(S["rstd0"], k + 1)
                dve.scalar_tensor_tensor(out=nb[:, 0], in0=mv[:, 0, :, 0], scalar=-1.0, in1=rstd[:, 0], op0=ALU.mult, op1=ALU.mult).then_inc(S["nb"], 1)

            def mid_stats(S, i, s):
                k = 2 * i + s
                dve.wait_ge(S["hT"], k + 1)
                wait(dve, S["msd"], k)
                wait(dve, S["midn"], k)
                dve.tensor_scalar(cnt_any[:], hTc[:, NT * P:NT * P + NT], 1.0, None, ALU.min)
                dve.tensor_scalar(cnt1[:], hTc[:, NT * P:NT * P + NT], 1.0, None, ALU.max).then_inc(S["any"], 1)
                dve.wait_ge(S["any"], k + 1)
                dve.reciprocal(inv_cnt[:], cnt1[:]).then_inc(S["cnt"], 1)
                dve.wait_ge(S["cnt"], k + 1)
                dve.wait_ge(S["prec"], k + 1)
                for j in range(NT):
                    last = dve.scalar_tensor_tensor(out=mid[:, j], in0=p_agg[:, j * F:(j + 1) * F], scalar=inv_cnt[:, j:j + 1],
                                                    in1=pre[:, j], op0=ALU.mult, op1=ALU.add)
                last.then_inc(S["midc"], 1)
                dve.wait_ge(S["midc"], k + 1)
                norm_stats(S, k, 1, [mid[:, j] for j in range(NT)], "stat1", "midv")

            def mid_norm(S, i, s):
                k = 2 * i + s
                dve.wait_ge(S["msd"], k + 1)
                dve.reciprocal(inv_sd[:], cnt_sd[:])
                dve.reciprocal(rstd[:, 1], sd[:, 1]).then_inc(S["rstd1"], 1)
                dve.wait_ge(S["rstd1"], k + 1)
                wait(dve, S["mT"], k)
                dve.tensor_tensor(deg_is[:, bass.ds(k * NT, NT)], inv_sd[:], cnt_any[:], ALU.mult)
                for j in range(NT):
                    last = dve.tensor_scalar(midn[:, j], mid[:, j], mv[:, 1, j, 0:1], rstd[:, 1, j:j + 1], ALU.subtract, ALU.mult)
                last.then_inc(S["midn"], 1)

            def prelu(S, i, s):
                k = 2 * i + s
                dve.wait_ge(S["pn"], k + 1)
                wait(dve, S["out"], k)
                dve.scalar_tensor_tensor(out=act_t, in0=neg, scalar=slope[:, 1:2], in1=pos, op0=ALU.mult, op1=ALU.add).then_inc(S["act"], 1)

            def x1_stats(S, i, s):
                k = 2 * i + s
                dve.wait_ge(S["out"], k + 1)
                dve.wait_ge(S["xb_in"][s], i * 16 + (16 * NT if isinstance(k, int) and k == NK - 1 else 16))
                wait(dve, S["x1_stored"][s], i * 16)
                wait(dve, S["h2"], k - 1)
                dve.tensor_tensor(x1[:, s], p_out[:, 0:NT * P].rearrange("p (j h) -> p j h", j=NT), xb[s], ALU.add).then_inc(S["x1c"], 1)
                dve.wait_ge(S["x1c"], k + 1)
                wait(dve, S["x1sd"], k)
                wait(dve, S["x1nb"], k)
                norm_stats(S, k, 2, [x1[:, s, j] for j in range(NT)], "stat2", "x1v")

            def x1_scale(S, i, s):
                k = 2 * i + s
                dve.wait_ge(S["x1sd"], k + 1)
                dve.wait_ge(S["midn"], k + 1)
                wait(dve, S["h2"], k)
                dve.reciprocal(rstd[:, 2], sd[:, 2]).then_inc(S["rstd2"], 1)
                dve.wait_ge(S["rstd2"], k + 1)
                dve.tensor_tensor(rstd[:, 2], rstd[:, 2], deg_is[:, bass.ds(k * NT, NT)], ALU.mult).then_inc(S["scale2"], 1)
                dve.wait_ge(S["scale2"], k + 1)
                dve.scalar_tensor_tensor(out=nb[:, 2], in0=mv[:, 2, :, 0], scalar=-1.0, in1=rstd[:, 2], op0=ALU.mult, op1=ALU.mult).then_inc(S["x1nb"], 1)

            step_ops = [(3, x_stats), (5, x_scale), (11, mid_stats), (13, mid_norm), (16, prelu), (18, x1_stats), (20, x1_scale)]

            dve.wait_ge(s_first, 32)
            dve.wait_ge(s_acc0, 1)
            run(dve, [(0, one_hot(0)), (1, lower), (5, add_window(0))], [], None)
            general_sums(0)
            run(dve, [], step_ops, S1)
            dve.wait_ge(S1["clear"], NK)
            run(dve, [(0, one_hot(1)), (2, add_window(1))], [], None)
            general_sums(1)

            def result_turn(i):
                for s in range(2):
                    if not isinstance(i, int) or 2 * i + s < NK:
                        k = 2 * i + s
                        dve.wait_ge(s_fT, k + 1)
                        dve.wait_ge(s_xl[s], i * 16 + 16)
                        wait(dve, s_st[s], i * 16)
                        for j in range(NT):
                            last = dve.scalar_tensor_tensor(out=x1[:, s, j], in0=(p_hT, p_mT)[s][:, j * P:(j + 1) * P],
                                                            scalar=deg_is[:, bass.ds(k * NT + j, 1)], in1=xb[s][:, j], op0=ALU.mult, op1=ALU.add)
                        last.then_inc(s_f, 1)
            turns(dve, result_turn, 2, K_END, K_ALL)


_INS = ['x', 'src', 'dst', 'edge_attr_128', 'L0_gnn_W1', 'L0_gnn_b1', 'L0_gnn_gamma', 'L0_gnn_beta', 'L0_gnn_prelu_a', 'L0_gnn_W2', 'L0_gnn_b2']


def kernel(**inputs):
    import numpy as _np
    import concourse.bacc as _bacc
    from concourse import mybir as _mybir
    from concourse.bass_utils import run_bass_kernel_spmd as _run

    nc = _bacc.Bacc("TRN2", target_bir_lowering=False, num_devices=1)
    arrays, args = {}, []
    for name in _INS:
        a = _np.ascontiguousarray(inputs[name])
        arrays[f"in_{name}_dram"] = a
        args.append(nc.dram_tensor(f"in_{name}_dram", a.shape, _mybir.dt.from_np(a.dtype), kind="ExternalInput").ap())
    n, h = inputs['x'].shape
    padded = -(-n // (NT * P)) * NT * P
    args.append(nc.dram_tensor("table", (padded, h), F32, kind="Internal").ap())
    args.append(nc.dram_tensor("x1_dram", (padded, h), F32, kind="Internal").ap())
    args.append(nc.dram_tensor("out_0_dram", (n, h), F32, kind="ExternalOutput").ap())
    gnn_kernel(nc, *args)
    r = _run(nc, [arrays], core_ids=[0])
    return r.results[0]["out_0_dram"]
```

```python
from contextlib import ExitStack

import concourse.bass as bass
from concourse import mybir

F32 = mybir.dt.float32
F32R = mybir.dt.float32r
BF16 = mybir.dt.bfloat16
I32 = mybir.dt.int32
ALU = mybir.AluOpType
ACT = mybir.ActivationFunctionType
AX_X = mybir.AxisListType.X

P = 128
T = 6
R = 3
W = 56
RING = 6
SPLIT = 4
FW = 4
SW = P + 2
NT = 2
POS = 12
STEP_AT = (0, 6)
SUB_DVE = 2
LAG_TURN_H, LAG_LINEAR2 = 9, 29
SHARE = (LAG_LINEAR2 - LAG_TURN_H) // (POS // 2)
CNT_AT = 64
EPS = 1e-5
PAD = -(1 << 20)


def gnn_kernel(nc, x, src, dst, attr, W1, b1, gamma, beta, prelu_a, W2, b2, table, x1_dram, out):
    N, H = x.shape
    E = attr.shape[0]
    F = W1.shape[1]
    assert H == P and F == 2 * P and W1.shape[0] == 2 * P
    GE = T * P
    CE = R * GE
    NC = -(-E // CE)
    NG = -(-E // GE)
    LAST = E - (NC - 1) * CE
    LAST_G = E - (NG - 1) * GE
    LAST_DMAS = (LAST_G >= T) + (LAST_G % T > 0)
    NK = -(-N // (NT * P))
    NTILES = NK * NT
    NOWHERE = NTILES * P
    NPAD = NOWHERE + W
    TAIL = N - (NTILES - 1) * P
    SE, SREST = E // P, E % P
    assert NC <= P and POS % RING == 0 and POS % SPLIT == 0 and 0 < TAIL <= P and NT == 2

    SAFE = 5
    G_END = NG // POS - 1
    K_END, K_ALL = (NK - 1) // 2, -(-NK // 2) + 4
    ALL = max(-(-(NG + 6) // POS), K_ALL + 1)
    assert SAFE < G_END <= K_END and K_END > SAFE

    def groups_for(i, s):
        return (i + 1) * POS + 3 * s
    NEED_A = 2 * NT * P * R // POS
    NEED_B = P
    assert all(NEED_A * (g // R) - NEED_B >= NT * P * (k + 1)
               for k in range(NK) for g in range(groups_for(k // 2, k % 2), NG)), "node steps are too early"

    with ExitStack() as ctx:
        def sb(name, shape, dt=F32):
            return ctx.enter_context(nc.sbuf_tensor(name, shape, dt))

        def bank(name):
            return ctx.enter_context(nc.psum_tensor(name, [P, 512], F32))

        def sem(name):
            return ctx.enter_context(nc.semaphore(name))

        sums_cnt = sb("sums_cnt", [P, 2, NPAD])
        acc = sums_cnt[:, 0]
        cnt = sums_cnt[0:1, 1]
        rows = sb("rows", [P, RING, T, P])
        split = sb("split", [P, SPLIT, 2, T, SW], F32R)
        hot = sb("hot", [P, SPLIT, T, W], F32R)
        local = sb("local", [P, NC * R, T])
        source = sb("source", [P, NC * R, T], I32)
        fw = sb("fw", [W, FW, SW])
        first = sb("first", [P, R])
        need_i = sb("need_i", [P, R], I32)
        need = sb("need", [P, R])
        good_first = sb("good_first", [P, 1])
        first_row = sb("first_row", [1, NG], I32)
        good = sb("good", [P, 1])
        flag = sb("flag", [1, 1], I32)
        index = sb("index", [P, RING, T], I32)
        ident = sb("ident", [P, P])
        iota_i = sb("iota_i", [P, W], I32)
        iota = sb("iota", [P, W])
        ones = sb("ones", [P, 1])
        ones_b = sb("ones_b", [P, P], BF16)
        zeros = sb("zeros", [P, NT * P])
        eps = sb("eps", [P, 1])
        w1 = sb("w1", [P, 2, F])
        w2 = sb("w2", [P, 2, P])
        bias = sb("bias", [P, F + P])
        bias_hi = sb("bias_hi", [P, F + P], BF16)
        bias_mid = sb("bias_mid", [P, F + P], BF16)
        bias_parts = sb("bias_parts", [P, F + P], BF16)
        gb = sb("gb", [P, 2, 2])
        gbn = sb("gbn", [P, 2, 2])
        slope = sb("slope", [P, 2])
        w2n = sb("w2n", [P, 2, P])
        deg_is = sb("deg_is", [P, NTILES])
        stats = sb("stats", [P, 3, NT, 6])
        mv = sb("mv", [P, 3, NT, 2])
        sd = sb("sd", [P, 3, NT])
        rstd = sb("rstd", [P, 3, NT])
        scale2 = sb("scale2", [P, NT])
        nb = sb("nb", [P, 3, NT])
        cnt1 = sb("cnt1", [P, NT])
        cnt_any = sb("cnt_any", [P, 2, NT])
        inv_cnt = sb("inv_cnt", [P, NT])
        cnt_sd = sb("cnt_sd", [P, NT])
        inv_sd = sb("inv_sd", [P, NT])
        cnt_row = sb("cnt_row", [1, NT * P])
        hTc = sb("hTc", [P, NT * P + NT])
        x1 = sb("x1", [P, 2, NT, P])
        h2 = sb("h2", [P, 2, NT, P])
        slow_dst = sb("slow_dst", [1, P], I32)
        slow_src = sb("slow_src", [P, 1], I32)

        work = sb("work", [P, 42 * P])
        raw = work[:, 0:CE].bitcast(I32)
        rawf = work[:, CE:2 * CE]
        inside = rows[:].rearrange("p a t h -> p (a t h)")[:, (RING - R) * GE:RING * GE]

        def part(at, a, b):
            return work[:, at * P:at * P + a * b].rearrange("p (a b) -> p a b", a=a)

        xa = [part(NT * u, NT, P) for u in range(2)]
        xb = [part(4 + NT * u, NT, P) for u in range(2)]
        agg = [part(8 + NT * u, NT, P) for u in range(2)]
        hb = part(12, NT, P)
        pre = part(14, NT, F)
        mid = part(18, NT, F)
        midn = part(22, NT, F)
        pos = [part(26 + 8 * u, 2 * NT, P) for u in range(2)]
        neg = [part(30 + 8 * u, 2 * NT, P) for u in range(2)]

        p_sum = [bank(f"p_sum{i}") for i in range(2)]
        p_wins = [bank(f"p_win{i}") for i in range(2)]
        p_win = p_wins[0]
        p_hT = bank("p_hT")
        p_pre = bank("p_pre")
        p_agg = bank("p_agg")
        p_mT = bank("p_mT")
        p_out = p_hT[:, 0:NT * P]

        s_fill = sem("raw_filled")
        s_raw = sem("raw_in")
        s_first = sem("first_row_in")
        s_const = sem("weights_in")
        s_ident = sem("ident_ready")
        s_iota = sem("iota_ready")
        s_ones = sem("ones_ready")
        s_gbn = sem("bias_parts_ready")
        s_rawf = sem("raw_as_float")
        s_turned = sem("raw_turned")
        s_local = sem("local_ready")
        s_source = sem("source_ready")
        s_good = sem("good_summed")
        s_flag = sem("flag_ready")
        s_acc0 = sem("acc_zeroed")
        s_chain = sem("dve_start_chain")
        s_rows = [[sem(f"rows{l}_in{i}") for i in range(RING)] for l in range(2)]
        s_hot = [sem(f"hot{l}_ready") for l in range(2)]
        s_win = [sem(f"window{l}_ready") for l in range(2)]
        s_add = [sem(f"window{l}_added") for l in range(2)]
        s_final = [sem(f"sums{l}_final") for l in range(2)]
        s_hi = sem("upper_ready")
        s_lo_d = sem("lower_ready_dve")
        s_lo_p = sem("lower_ready_pool")
        s_sum = sem("group_summed")
        s_fw = sem("group_copied")
        s_index = sem("index_ready")
        s_gd = [sem(f"general{l}_dst_in") for l in range(2)]
        s_gi = sem("general_src_in")
        s_gr = [sem(f"general{l}_rows_in") for l in range(2)]
        s_gt = [sem(f"general{l}_turned") for l in range(2)]
        s_ga = [sem(f"general{l}_added") for l in range(2)]

        STEP_SEMS = ("agg cntr clear stat0 var sd rstd0 nb h hTp hT pre prec any some csd cnt midc stat1 midv msd rstd1 midn mT pn "
                     "out x1c stat2 x1v x1sd rstd2 scale2 x1nb h2").split()

        def step_sems(tag):
            S = {name: sem(f"{tag}_{name}") for name in STEP_SEMS}
            for name in ("xa_in", "xb_in", "x1_stored", "h2_stored"):
                S[name] = [sem(f"{tag}_{name}{u}") for u in range(2)]
            return S

        def result_sems(tag):
            S = {name: sem(f"{tag}_{name}") for name in ("moved", "turned", "added")}
            for name in ("x1_in", "stored"):
                S[name] = [sem(f"{tag}_{name}{u}") for u in range(2)]
            return S

        block = ctx.enter_context(nc.Block())

        def wait(eng, s, value):
            if not isinstance(value, int) or value > 0:
                eng.wait_ge(s, value)

        def turns(eng, turn, safe, end, total):
            for i in range(safe):
                turn(i)
            with eng.Fori(safe, end) as i:
                turn(i)
            for i in range(end, total):
                turn(i)

        def run(eng, group_ops, step_ops, S, beside=False):
            beside = beside or len(group_ops) > 0
            late = POS if beside else 0

            def turn(i):
                for p in range(POS):
                    for lag, f in group_ops:
                        gi, gp = i + (p - lag) // POS, (p - lag) % POS
                        if not isinstance(gi, int) or 0 <= gi * POS + gp < NG:
                            f(gi, gp)
                    for lag, f in reversed(step_ops):
                        for s in range(2):
                            back, rest = divmod(p - STEP_AT[s] - lag - late, POS)
                            ki = i + back
                            if rest == 0 and (not isinstance(ki, int) or 0 <= 2 * ki + s < NK):
                                f(S, ki, s)
            if min([lag for lag, f in group_ops + step_ops]) < 0:
                turn(-1)
            if beside:
                turns(eng, turn, SAFE, G_END, ALL)
            else:
                turns(eng, turn, SAFE, K_END, K_ALL)

        def slot_steps(u):
            return (NK - u + 1) // 2

        def pass_over(eng, S):
            eng.wait_ge(S["h2"], NK)
            eng.wait_ge(S["clear"], NK)
            for u in range(2):
                eng.wait_ge(S["x1_stored"][u], 16 * slot_steps(u))
                eng.wait_ge(S["h2_stored"][u], 16 * slot_steps(u))

        def result_over(eng, S):
            for u in range(2):
                eng.wait_ge(S["stored"][u], 16 * (slot_steps(u) + (NT - 1 if u == (NK - 1) % 2 else 0)))

        def general(eng):
            eng.wait_ge(s_flag, 1)
            return eng.value_load(flag[0:1, 0:1], min_val=0, max_val=1)

        def node_rows(dram, k):
            return dram[bass.ds(k * (NT * P), NT * P)].rearrange("(j p) h -> p j h", p=P)

        S1 = step_sems("n")
        S2 = step_sems("g")
        R1 = result_sems("r")
        R2 = result_sems("rg")

        @block.sync
        def _(sp):
            body = (NC - 1) * CE
            for n, edges in enumerate((dst, src)):
                sp.wait_ge(s_fill, n + 1)
                sp.dma_start(raw[0:NC - 1, :], edges[0:body].rearrange("(c e) -> c e", e=CE)).then_inc(s_raw, 16)
                sp.dma_start(raw[NC - 1:NC, 0:LAST], edges[body:E].rearrange("(c e) -> c e", c=1)).then_inc(s_raw, 16)
                if n == 0:
                    with nc.allow_non_contiguous_dma(reason="one value of each group"):
                        whole = GE * (NG - 1)
                        sp.dma_start(first_row[0:1, 0:NG - 1], dst[0:whole].rearrange("(g e) -> e g", e=GE)[0:1, :]).then_inc(s_first, 16)
                        sp.dma_start(first_row[0:1, NG - 1:NG], dst[whole:whole + 1].rearrange("(g e) -> e g", e=1)).then_inc(s_first, 16)

            def load_rows(i, p):
                g, slot = i * POS + p, p % RING
                if isinstance(g, int) and g == RING - R:
                    sp.wait_ge(s_good, 1)
                wait(sp, s_lo_d, g - RING + 1)
                wait(sp, s_lo_p, g - RING + 1)
                if isinstance(g, int) and g == NG - 1:
                    e, full = g * GE, LAST_G // T
                    if full:
                        sp.dma_start(rows[0:full, slot].rearrange("p t h -> p (t h)"),
                                     attr[e:e + full * T].rearrange("(p t) h -> p (t h)", t=T)).then_inc(s_rows[0][slot], 16)
                    if LAST_G % T:
                        sp.dma_start(rows[full:full + 1, slot, 0:LAST_G % T].rearrange("p t h -> p (t h)"),
                                     attr[e + full * T:E].rearrange("(p t) h -> p (t h)", p=1)).then_inc(s_rows[0][slot], 16)
                else:
                    sp.dma_start(rows[:, slot].rearrange("p t h -> p (t h)"),
                                 attr[bass.ds(g * GE, GE)].rearrange("(p t) h -> p (t h)", t=T)).then_inc(s_rows[0][slot], 16)

            def load_x(into, landed, freed):
                def f(S, i, s):
                    k = 2 * i + s
                    if isinstance(k, int) and k == 0:
                        sp.wait_ge(s_source, 1)
                    wait(sp, S[freed], k - 1)
                    if isinstance(k, int) and k == NK - 1:
                        for j in range(NT):
                            n, m = (k * NT + j) * P, P if j < NT - 1 else TAIL
                            sp.dma_start(into[s][0:m, j], x[n:n + m]).then_inc(S[landed][s], 16)
                    else:
                        sp.dma_start(into[s], node_rows(x, k)).then_inc(S[landed][s], 16)
                return f

            def store_nodes(S, i, s):
                k = 2 * i + s
                sp.wait_ge(S["h2"], k + 1)
                sp.dma_start(node_rows(table, k), h2[:, s]).then_inc(S["h2_stored"][s], 16)
                sp.dma_start(node_rows(x1_dram, k), x1[:, s]).then_inc(S["x1_stored"][s], 16)

            step_ops = [(0, load_x(xa, "xa_in", "h")), (26, load_x(xb, "xb_in", "x1c")), (39, store_nodes)]
            run(sp, [(-4, load_rows)], step_ops, S1)

            def slow_tiles(layer):
                def slow_tile(t, n):
                    sp.wait_ge(s_ga[layer], t + 1)
                    sp.dma_start(slow_dst[0:1, 0:n], dst[bass.ds(t * P, n)].rearrange("(a e) -> a e", a=1)).then_inc(s_gd[layer], 16)
                    if layer == 0:
                        sp.dma_start(rows[0:n, 0, 0, :], attr[bass.ds(t * P, n)]).then_inc(s_gr[0], 16)
                    else:
                        sp.dma_start(slow_src[0:n, :], src[bass.ds(t * P, n)].rearrange("(e a) -> e a", a=1)).then_inc(s_gi, 16)
                with sp.Fori(0, SE) as t:
                    slow_tile(t, P)
                if SREST:
                    slow_tile(SE, SREST)

            with sp.If(general(sp) > 0):
                pass_over(sp, S1)
                slow_tiles(0)
                run(sp, [], step_ops, S2)
                pass_over(sp, S2)
            pass_over(sp, S1)

            def load_x1(S, i, s):
                k = 2 * i + s
                wait(sp, S["added"], k - 1)
                sp.dma_start(xb[s], node_rows(x1_dram, k)).then_inc(S["x1_in"][s], 16)

            def store_out(S, i, s):
                k = 2 * i + s
                sp.wait_ge(S["added"], k + 1)
                if isinstance(k, int) and k == NK - 1:
                    for j in range(NT):
                        n, m = (k * NT + j) * P, P if j < NT - 1 else TAIL
                        sp.dma_start(out[n:n + m], x1[0:m, s, j]).then_inc(S["stored"][s], 16)
                else:
                    sp.dma_start(node_rows(out, k), x1[:, s]).then_inc(S["stored"][s], 16)

            run(sp, [], [(-4, load_x1), (8, store_out)], R1, beside=True)
            result_over(sp, R1)
            with sp.If(general(sp) > 0):
                slow_tiles(1)
                run(sp, [], [(0, load_x1), (8, store_out)], R2)
                result_over(sp, R2)

        @block.gpsimd
        def _(pool):
            pool.memset(ident[:], 0.0).then_inc(s_ident, 1)
            pool.wait_ge(s_ident, 1)
            pool.affine_select(out=ident[:], in_=ident[:], compare_op=ALU.not_equal, fill=1.0, base=0,
                               pattern=[[-1, P]], channel_multiplier=1).then_inc(s_ident, 1)
            pool.iota(need_i[:], pattern=[[0, R]], base=-NEED_B, channel_multiplier=NEED_A)
            pool.iota(iota_i[:], pattern=[[1, W]], base=0, channel_multiplier=0).then_inc(s_iota, 1)
            pool.memset(zeros[:], 0.0)
            pool.memset(sums_cnt[:], 0.0).then_inc(s_acc0, 1)

            def lower(i, p):
                g = i * POS + p
                pool.wait_ge(s_hi, g + 1)
                pool.tensor_tensor(split[:, p % SPLIT, 1, SUB_DVE:T, 0:P], rows[:, p % RING, SUB_DVE:T],
                                   split[:, p % SPLIT, 0, SUB_DVE:T, 0:P].bitcast(F32), ALU.subtract).then_inc(s_lo_p, 1)

            def move_agg(S, i, s):
                k = 2 * i + s
                if S is S1:
                    n = groups_for(i, s)
                    pool.wait_ge(s_add[0], min(n, NG) if isinstance(n, int) else n)
                wait(pool, S["pre"], k - 1)
                nodes = acc[:, bass.ds(k * (NT * P), NT * P)]
                pool.nop(nofuse=True)
                pool.tensor_tensor(agg[s].rearrange("p j h -> p (j h)"), nodes, zeros[:], ALU.add).then_inc(S["agg"], 1)

            def move_counts(S, i, s):
                k = 2 * i + s
                wait(pool, S["hTp"], k)
                pool.nop(nofuse=True)
                pool.tensor_tensor(cnt_row[:], cnt[0:1, bass.ds(k * (NT * P), NT * P)], zeros[0:1, :], ALU.add).then_inc(S["cntr"], 1)

            def clear_acc(S, i, s):
                k = 2 * i + s
                pool.wait_ge(S["agg"], k + 1)
                pool.nop(nofuse=True)
                pool.tensor_tensor(acc[:, bass.ds(k * (NT * P), NT * P)], zeros[:], zeros[:], ALU.add).then_inc(S["clear"], 1)

            step_ops = [(7, move_agg), (8, move_counts), (9, clear_acc)]
            run(pool, [(1, lower)], step_ops, S1)
            with pool.If(general(pool) > 0):
                pass_over(pool, S1)
                pool.wait_ge(s_final[0], 1)
                run(pool, [], step_ops, S2)
                pass_over(pool, S2)
            pass_over(pool, S1)

            def gather(i, p):
                g, slot = i * POS + p, p % RING
                pool.wait_ge(s_index, g + 1)
                wait(pool, s_win[1], g - RING + 1)
                pool.nop(nofuse=True)
                for t in range(T):
                    pool.indirect_dma_start(rows[:, slot, t], None, table,
                                            bass.IndirectOffsetOnAxis(ap=index[:, slot, t:t + 1], axis=0)).then_inc(s_rows[1][slot], 16)
            run(pool, [(0, gather)], [], None)

            with pool.If(general(pool) > 0):
                def slow_tile(t, n):
                    pool.wait_ge(s_gi, 16 * t + 16)
                    pool.nop(nofuse=True)
                    pool.indirect_dma_start(rows[0:n, 0, 0, :], None, table,
                                            bass.IndirectOffsetOnAxis(ap=slow_src[0:n, 0:1], axis=0)).then_inc(s_gr[1], 16)
                with pool.Fori(0, SE) as t:
                    slow_tile(t, P)
                if SREST:
                    slow_tile(SE, SREST)

        @block.scalar
        def _(act):
            act.dma_start(w1[:], W1.rearrange("(a p) f -> p a f", p=P)).then_inc(s_const, 16)
            act.dma_start(w2[:], W2.rearrange("(a p) h -> p a h", p=P)).then_inc(s_const, 16)
            act.dma_start(bias[:, 0:F], b1.rearrange("(a f) -> a f", a=1).to_broadcast([P, F])).then_inc(s_const, 16)
            act.dma_start(bias[:, F:F + P], b2.rearrange("(a f) -> a f", a=1).to_broadcast([P, P])).then_inc(s_const, 16)
            with nc.allow_non_contiguous_dma(reason="512 single values"):
                act.dma_start(gb[:, 0, :], gamma.rearrange("(a p) -> p a", p=P)).then_inc(s_const, 16)
                act.dma_start(gb[:, 1, :], beta.rearrange("(a p) -> p a", p=P)).then_inc(s_const, 16)
            act.dma_start(slope[:, 0:1], prelu_a.rearrange("(a f) -> a f", a=1).to_broadcast([P, 1])).then_inc(s_const, 16)

            def upper(i, p):
                g = i * POS + p
                act.wait_ge(s_rows[0][p % RING], (i * (POS // RING) + p // RING) * 16 + (16 * LAST_DMAS if isinstance(g, int) and g == NG - 1 else 16))
                wait(act, s_sum, g - SPLIT + 1)
                act.copy(split[:, p % SPLIT, 0, :, 0:P], rows[:, p % RING]).then_inc(s_hi, 1)

            def copy_sums(i, p):
                g = i * POS + p
                act.wait_ge(s_sum, g + 1)
                wait(act, s_win[0], g - FW + 1)
                act.copy(fw[:, p % FW], p_sum[p % 2][0:W, 0:SW]).then_inc(s_fw, 1)

            def x_sd(S, i, s):
                k = 2 * i + s
                act.wait_ge(S["var"], k + 1)
                wait(act, S["rstd0"], k)
                act.activation(sd[:, 0], mv[:, 0, :, 1], ACT.Sqrt, bias=eps[:, 0:1]).then_inc(S["sd"], 1)

            def norm_x(S, i, s):
                k = 2 * i + s
                act.wait_ge(S["nb"], k + 1)
                wait(act, S["hTp"], k)
                for j in range(NT):
                    last = act.activation(hb[:, j], xa[s][:, j], ACT.Relu, scale=rstd[:, 0, j:j + 1], bias=nb[:, 0, j:j + 1])
                last.then_inc(S["h"], 1)

            def copy_hT(S, i, s):
                k = 2 * i + s
                act.wait_ge(S["hTp"], k + 1)
                wait(act, S["pre"], k)
                wait(act, S["some"], k)
                wait(act, S["any"], k)
                act.copy(hTc[:], p_hT[:, 0:NT * P + NT]).then_inc(S["hT"], 1)

            def copy_pre(S, i, s):
                k = 2 * i + s
                act.wait_ge(S["pre"], k + 1)
                wait(act, S["midc"], k)
                act.copy(pre, p_pre[:, :].rearrange("p (j f) -> p j f", j=NT)).then_inc(S["prec"], 1)
                act.wait_ge(S["any"], k + 1)
                wait(act, S["rstd1"], k)
                act.activation(cnt_sd[:], cnt1[:], ACT.Sqrt).then_inc(S["csd"], 1)

            def mid_sd(S, i, s):
                k = 2 * i + s
                act.wait_ge(S["midv"], k + 1)
                wait(act, S["rstd1"], k)
                act.activation(sd[:, 1], mv[:, 1, :, 1], ACT.Sqrt, bias=eps[:, 0:1]).then_inc(S["msd"], 1)

            def relus(a):
                def f(S, i, s):
                    k = 2 * i + s
                    act.wait_ge(S["mT"], k + 1)
                    wait(act, S["out"], k - 1)
                    t = p_mT[:, a * NT * P:(a + 1) * NT * P].rearrange("p (j h) -> p j h", j=NT)
                    act.activation(pos[s][:, a * NT:(a + 1) * NT], t, ACT.Relu, scale=gb[:, 0, a:a + 1], bias=gb[:, 1, a:a + 1])
                    act.activation(neg[s][:, a * NT:(a + 1) * NT], t, ACT.Relu, scale=gbn[:, 0, a:a + 1], bias=gbn[:, 1, a:a + 1]).then_inc(S["pn"], 1)
                return f

            def x1_sd(S, i, s):
                k = 2 * i + s
                act.wait_ge(S["x1v"], k + 1)
                wait(act, S["rstd2"], k)
                act.activation(sd[:, 2], mv[:, 2, :, 1], ACT.Sqrt, bias=eps[:, 0:1]).then_inc(S["x1sd"], 1)

            def norm_x1(S, i, s):
                k = 2 * i + s
                act.wait_ge(S["x1nb"], k + 1)
                wait(act, S["h2_stored"][s], i * 16)
                for j in range(NT):
                    last = act.activation(h2[:, s, j], x1[:, s, j], ACT.Relu, scale=scale2[:, j:j + 1], bias=nb[:, 2, j:j + 1])
                last.then_inc(S["h2"], 1)

            step_ops = [(4, x_sd), (8, norm_x), (10, copy_hT), (15, copy_pre), (19, mid_sd), (23, relus(0)), (24, relus(1)), (34, x1_sd), (38, norm_x1)]
            act.wait_ge(s_ones, 1)
            act.activation(sd[:, 0], eps[:, 0:1].to_broadcast([P, NT]), ACT.Sqrt)
            act.wait_ge(s_gbn, 1)
            run(act, [(3, copy_sums), (0, upper)], step_ops, S1)
            with act.If(general(act) > 0):
                pass_over(act, S1)
                run(act, [], step_ops, S2)
                pass_over(act, S2)
            pass_over(act, S1)

            act.wait_ge(s_source, 1)

            def copy_index(i, p):
                slot = p % RING
                wait(act, s_rows[1][slot], (i * (POS // RING) + p // RING) * (16 * T))
                act.copy(index[:, slot], source[:, bass.ds(i * POS + p, 1), :].rearrange("p g t -> p (g t)")).then_inc(s_index, 1)

            def move_sums(S, i, s):
                k = 2 * i + s
                if S is R1:
                    n = groups_for(i, s)
                    act.wait_ge(s_add[1], min(n, NG) if isinstance(n, int) else n)
                wait(act, S["turned"], k - 1)
                act.copy(agg[s].rearrange("p j h -> p (j h)"), acc[:, bass.ds(k * (NT * P), NT * P)]).then_inc(S["moved"], 1)

            run(act, [(0, copy_index)], [(3, move_sums)], R1)
            with act.If(general(act) > 0):
                act.wait_ge(s_final[1], 1)
                run(act, [], [(3, move_sums)], R2)

        @block.tensor
        def _(pe):
            banks = [p_hT, p_pre, p_agg, p_mT, p_wins[1]]

            def turn_raw():
                for rt in range(R * T):
                    r, t = rt // T, rt % T
                    v = rawf[0:NC, r * GE:(r + 1) * GE].rearrange("c (p t) -> c t p", t=T)[:, t, :]
                    last = pe.transpose(banks[rt // 4][:, (rt % 4) * P:(rt % 4) * P + NC], v, ident[0:NC, 0:NC])
                last.then_inc(s_turned, 1)

            pe.wait_ge(s_ident, 2)
            pe.wait_ge(s_rawf, 1)
            turn_raw()
            pe.wait_ge(s_good, 1)
            pe.matmul(p_win[0:1, 0:1], good_first[0:NC, 0:1], ones[0:NC, 0:1], start=True, stop=False)
            pe.matmul(p_win[0:1, 0:1], good[0:NC, 0:1], ones[0:NC, 0:1], start=False, stop=True).then_inc(s_good, 1)
            pe.wait_ge(s_rawf, 2)
            pe.wait_ge(s_local, 1)
            turn_raw()
            pe.wait_ge(s_flag, 1)
            pe.wait_ge(s_ones, 2)

            def sums(i, p):
                g = i * POS + p
                pe.wait_ge(s_hot[0], g + 1)
                pe.wait_ge(s_hi, g + 1)
                pe.wait_ge(s_lo_d, g + 1)
                pe.wait_ge(s_lo_p, g + 1)
                wait(pe, s_fw, g - 1)
                for t in range(T):
                    for h in range(2):
                        last = pe.matmul(p_sum[p % 2][0:W, 0:SW], hot[:, p % SPLIT, t], split[:, p % SPLIT, h, t],
                                         start=(t == 0 and h == 0), stop=(t == T - 1 and h == 1))
                last.then_inc(s_sum, 1)

            def turn_window(i, p):
                g = i * POS + p
                pe.wait_ge(s_fw, g + 1)
                wait(pe, s_add[0], g - 1)
                pe.nop(nofuse=True)
                pe.transpose(p_wins[p % 2][:, 0:W], fw[:, p % FW, 0:P], ident[0:W, 0:W])
                pe.transpose(p_wins[p % 2][0:2, CNT_AT:CNT_AT + W], fw[:, p % FW, P:SW], ident[0:W, 0:W]).then_inc(s_win[0], 1)

            def turn_h(S, i, s):
                k = 2 * i + s
                pe.wait_ge(S["h"], k + 1)
                pe.wait_ge(S["cntr"], k + 1)
                wait(pe, S["hT"], k)
                wait(pe, S["x1c"], k - SHARE)
                for j in range(NT):
                    pe.transpose(p_hT[:, j * P:(j + 1) * P], hb[:, j], ident[:])
                for j in range(NT):
                    last = pe.matmul(p_hT[:, NT * P + j:NT * P + j + 1], cnt_row[0:1, j * P:(j + 1) * P], ones[0:1, 0:1], start=True, stop=True)
                last.then_inc(S["hTp"], 1)

            def linear1(j):
                def f(S, i, s):
                    k = 2 * i + s
                    if j == 0:
                        pe.wait_ge(S["hT"], k + 1)
                        pe.wait_ge(S["agg"], k + 1)
                        wait(pe, S["prec"], k)
                        wait(pe, S["midc"], k)
                    o = p_pre[:, j * F:(j + 1) * F]
                    pe.matmul(o, ones_b[:, :], bias_parts[:, 0:F], start=True, stop=False)
                    pe.matmul(o, hTc[:, j * P:(j + 1) * P], w1[:, 0], start=False, stop=True)
                    last = pe.matmul(p_agg[:, j * F:(j + 1) * F], agg[s][:, j], w1[:, 1], start=True, stop=True)
                    if j == NT - 1:
                        last.then_inc(S["pre"], 1)
                return f

            def turn_mid(S, i, s):
                k = 2 * i + s
                pe.wait_ge(S["midn"], k + 1)
                wait(pe, S["pn"], 2 * k)
                for a in range(2):
                    for j in range(NT):
                        last = pe.transpose(p_mT[:, (a * NT + j) * P:(a * NT + j + 1) * P], midn[:, j, a * P:(a + 1) * P], ident[:])
                last.then_inc(S["mT"], 1)

            def linear2(j):
                def f(S, i, s):
                    k = 2 * i + s
                    if j == 0:
                        pe.wait_ge(S["pn"], 2 * k + 2)
                        wait(pe, S["x1c"], k)
                        n = k + SHARE + 1
                        pe.wait_ge(S["hT"], min(n, NK) if isinstance(n, int) else n)
                    o = p_out[:, j * P:(j + 1) * P]
                    pe.matmul(o, ones_b[:, :], bias_parts[:, F:F + P], start=True, stop=False)
                    for a in range(2):
                        pe.matmul(o, pos[s][:, a * NT + j], w2[:, a], start=False, stop=False)
                        last = pe.matmul(o, neg[s][:, a * NT + j], w2n[:, a], start=False, stop=(a == 1))
                    if j == NT - 1:
                        last.then_inc(S["out"], 1)
                return f

            step_ops = [(LAG_TURN_H, turn_h), (13, linear1(0)), (14, linear1(1)), (22, turn_mid), (LAG_LINEAR2, linear2(0)), (LAG_LINEAR2 + 1, linear2(1))]

            def general_sums(layer):
                def slow_tile(t, n):
                    pe.wait_ge(s_gr[layer], 16 * t + 16)
                    pe.wait_ge(s_ga[layer], t + 1)
                    pe.transpose(p_win[:, 0:n], rows[0:n, 0, 0, :], ident[0:n, 0:n]).then_inc(s_gt[layer], 1)
                with pe.Fori(0, SE) as t:
                    slow_tile(t, P)
                if SREST:
                    slow_tile(SE, SREST)

            pe.wait_ge(s_gbn, 1)
            pe.wait_ge(s_const, 16 * 7)
            run(pe, [(5, turn_window), (2, sums)], step_ops, S1)
            with pe.If(general(pe) > 0):
                general_sums(0)
                run(pe, [], step_ops, S2)
                pass_over(pe, S2)
            pass_over(pe, S1)

            def gathered_sums(i, p):
                g = i * POS + p
                pe.wait_ge(s_hot[1], g + 1)
                pe.wait_ge(s_rows[1][p % RING], (i * (POS // RING) + p // RING) * (16 * T) + 16 * T)
                wait(pe, s_add[1], g - 1)
                for t in range(T):
                    last = pe.matmul(p_sum[p % 2][:, 0:W], rows[:, p % RING, t], hot[:, p % SPLIT, t].bitcast(F32), start=(t == 0), stop=(t == T - 1))
                last.then_inc(s_win[1], 1)

            def turn_sums(S, i, s):
                k = 2 * i + s
                pe.wait_ge(S["moved"], k + 1)
                wait(pe, S["added"], k - 1)
                for j in range(NT):
                    last = pe.transpose((p_hT, p_mT)[s][:, j * P:(j + 1) * P], agg[s][:, j], ident[:])
                last.then_inc(S["turned"], 1)

            run(pe, [(0, gathered_sums)], [(4, turn_sums)], R1)
            with pe.If(general(pe) > 0):
                general_sums(1)
                run(pe, [], [(4, turn_sums)], R2)

        @block.vector
        def _(dve):
            links = [0]

            def link(ins):
                links[0] += 1
                ins.then_inc(s_chain, 1)
                dve.wait_ge(s_chain, links[0])

            def fill(value):
                return dve.memset(raw[NC // 32 * 32:P, LAST:CE], value)
            fill(PAD).then_inc(s_fill, 1)
            dve.memset(ones[:], 1.0)
            dve.memset(ones_b[:], 1.0)
            dve.memset(bias_parts[:], 0.0)
            dve.memset(eps[:], EPS).then_inc(s_ones, 1)
            dve.wait_ge(s_iota, 1)
            dve.tensor_copy(iota[:], iota_i[:])
            dve.tensor_copy(need[:], need_i[:])
            dve.wait_ge(s_raw, 32)
            link(dve.tensor_copy(rawf[0:NC], raw[0:NC]))
            dve.tensor_scalar(first[0:NC], rawf[0:NC].rearrange("c (r e) -> c e r", r=R)[:, 0, :], 0.0, None, ALU.max)
            link(fill(0))
            dve.sem_inc(s_fill, 1)
            for r in range(R):
                last = dve.tensor_scalar(rawf[0:NC, r * GE:(r + 1) * GE], rawf[0:NC, r * GE:(r + 1) * GE], first[0:NC, r:r + 1], None, ALU.subtract)
            link(last)
            dve.sem_inc(s_rawf, 1)
            dve.tensor_tensor(need[0:NC], first[0:NC], need[0:NC], ALU.is_ge)
            link(dve.tensor_scalar(inside[0:NC], rawf[0:NC], 0.0, None, ALU.is_ge))
            dve.tensor_reduce(good_first[0:NC], need[0:NC], AX_X, ALU.add)
            link(dve.scalar_tensor_tensor(out=inside[0:NC], in0=rawf[0:NC], scalar=float(W), in1=inside[0:NC], op0=ALU.is_lt, op1=ALU.mult))
            dve.tensor_reduce(good[0:NC], inside[0:NC], AX_X, ALU.add).then_inc(s_good, 1)

            def take_turned(into):
                v = into[:].rearrange("p (c r) t -> p c (r t)", r=R)
                for b, bank_ in enumerate((p_hT, p_pre, p_agg, p_mT, p_wins[1])):
                    n = min(4, R * T - 4 * b)
                    last = dve.tensor_copy(v[:, :, 4 * b:4 * b + n].rearrange("p c t -> p t c"),
                                           bank_[:, :].rearrange("p (t c) -> p t c", c=P)[:, 0:n, 0:NC])
                return last
            dve.wait_ge(s_turned, 1)
            take_turned(local).then_inc(s_local, 1)
            dve.wait_ge(s_good, 2)
            for h in range(2):
                v = split[:].bitcast(F32)[:, :, h, :, P:SW]
                last = dve.memset(v, 0.0)
            link(last)
            for b in range(SPLIT):
                last = dve.memset(split[:].bitcast(F32)[:, b, 0, :, P:P + 1], 1.0)
            last.then_inc(s_ones, 1)
            link(dve.tensor_scalar(good[0:1, :], p_win[0:1, 0:1], -1.0, float(E + NG), ALU.mult, ALU.add))
            dve.tensor_scalar(flag[:], good[0:1, :], 1.0, None, ALU.min).then_inc(s_flag, 1)
            link(dve.tensor_scalar(good[0:1, :], good[0:1, :], 1.0, float(NOWHERE), ALU.min, ALU.mult))
            dve.wait_ge(s_first, 32)
            link(dve.tensor_scalar(first_row[:], first_row[:], good[0:1, 0:1], None, ALU.max))
            dve.wait_ge(s_raw, 64)
            link(dve.tensor_copy(rawf[0:NC], raw[0:NC]))
            dve.sem_inc(s_rawf, 1)
            dve.wait_ge(s_turned, 2)
            take_turned(source).then_inc(s_source, 1)
            dve.wait_ge(s_source, 1)
            for w in p_wins:
                dve.memset(w[:, CNT_AT:CNT_AT + W], 0.0)
            dve.wait_ge(s_const, 16 * 7)
            link(dve.tensor_copy(bias_hi[:], bias[:]))
            link(dve.tensor_tensor(bias[:], bias[:], bias_hi[:], ALU.subtract))
            link(dve.tensor_copy(bias_mid[:], bias[:]))
            dve.tensor_copy(bias_parts[0:1, :], bias_hi[0:1, :])
            dve.tensor_copy(bias_parts[32:33, :], bias_mid[32:33, :])
            dve.tensor_tensor(bias_parts[64:65, :], bias[64:65, :], bias_mid[64:65, :], ALU.subtract)
            dve.tensor_scalar(gbn[:], gb[:], -1.0, None, ALU.mult)
            link(dve.tensor_scalar(slope[:, 1:2], slope[:, 0:1], -1.0, None, ALU.mult))
            dve.tensor_scalar(w2n[:], w2[:], slope[:, 1:2], None, ALU.mult).then_inc(s_gbn, 1)

            def one_hot(layer):
                used = s_sum if layer == 0 else s_win[1]

                def f(i, p):
                    g = i * POS + p
                    wait(dve, used, g - SPLIT + 1)
                    dve.tensor_tensor(hot[:, p % SPLIT], local[:, bass.ds(g, 1), :].rearrange("p g t -> p (g t)").to_broadcast([P, T, W]),
                                      iota[:].rearrange("p (a w) -> p a w", a=1).to_broadcast([P, T, W]), ALU.is_equal).then_inc(s_hot[layer], 1)
                return f

            def lower(i, p):
                g = i * POS + p
                dve.wait_ge(s_hi, g + 1)
                dve.tensor_tensor(split[:, p % SPLIT, 1, 0:SUB_DVE, 0:P], rows[:, p % RING, 0:SUB_DVE],
                                  split[:, p % SPLIT, 0, 0:SUB_DVE, 0:P].bitcast(F32), ALU.subtract).then_inc(s_lo_d, 1)

            def load_nodes(count):
                def f(i, p):
                    if p % count == 0:
                        g = i * POS + p
                        n = min(count, NG - g) if isinstance(g, int) else count
                        _, values = nc.values_load_multi_w_load_instructions(first_row[0:1, bass.ds(g, n)], engines=[mybir.EngineType.DVE],
                                                                             min_val=0, max_val=NOWHERE)
                        for m in range(n):
                            nodes[p + m] = values[m]
                return f
            nodes = {}

            def add_window(layer):
                def f(i, p):
                    g = i * POS + p
                    node = nodes[p]
                    dve.wait_ge(s_win[layer], g + 1)
                    wait(dve, s_add[layer], g)
                    if layer == 0:
                        place = sums_cnt[:, :, bass.ds(node, W)]
                        window = p_wins[p % 2][:, 0:2 * CNT_AT].rearrange("p (a w) -> p a w", a=2)[:, :, 0:W]
                    else:
                        place = acc[:, bass.ds(node, W)]
                        window = p_sum[p % 2][:, 0:W]
                    dve.tensor_tensor(place, window, place, ALU.add).then_inc(s_add[layer], 1)
                return f

            def general_sums(layer):
                dve.memset(acc, 0.0)
                if layer == 0:
                    dve.memset(cnt, 0.0)
                dve.drain().then_inc(s_ga[layer], 1)

                def slow_tile(t, n):
                    dve.wait_ge(s_gd[layer], 16 * t + 16)
                    dve.wait_ge(s_gt[layer], t + 1)
                    dve.nop(nofuse=True)
                    with dve.Fori(0, n) as e:
                        node = dve.value_load(slow_dst[0:1, bass.ds(e, 1)], min_val=0, max_val=N - 1)
                        place = acc[:, bass.ds(node, 1)]
                        dve.tensor_tensor(place, p_win[:, bass.ds(e, 1)], place, ALU.add)
                        if layer == 0:
                            one = cnt[0:1, bass.ds(node, 1)]
                            dve.tensor_scalar(one, one, 1.0, None, ALU.add)
                        dve.drain()
                    dve.drain().then_inc(s_ga[layer], 1)
                with dve.Fori(0, SE) as t:
                    slow_tile(t, P)
                if SREST:
                    slow_tile(SE, SREST)
                dve.sem_inc(s_final[layer], 1)

            def aggregate(which, stat, done, *read):
                def f(S, i, s):
                    k = 2 * i + s
                    dve.wait_ge(S[stat], k + 1)
                    for r in read:
                        wait(dve, S[r], k)
                    dve.nop(nofuse=True)
                    for j in range(NT):
                        last = dve.bn_aggr(mv[:, which, j], stats[:, which, j])
                    last.then_inc(S[done], 1)
                return f

            def x_stats(S, i, s):
                k = 2 * i + s
                dve.wait_ge(S["xa_in"][s], i * 16 + (16 * NT if isinstance(k, int) and k == NK - 1 else 16))
                wait(dve, S["var"], k)
                for j in range(NT):
                    last = dve.bn_stats(stats[:, 0, j], xa[s][:, j])
                last.then_inc(S["stat0"], 1)

            def x_scale(S, i, s):
                k = 2 * i + s
                dve.wait_ge(S["sd"], k + 1)
                wait(dve, S["h"], k)
                dve.reciprocal(rstd[:, 0], sd[:, 0]).then_inc(S["rstd0"], 1)

            def x_shift(S, i, s):
                k = 2 * i + s
                dve.wait_ge(S["rstd0"], k + 1)
                dve.scalar_tensor_tensor(out=nb[:, 0], in0=mv[:, 0, :, 0], scalar=-1.0, in1=rstd[:, 0], op0=ALU.mult, op1=ALU.mult).then_inc(S["nb"], 1)

            def count_max(S, i, s):
                k = 2 * i + s
                dve.wait_ge(S["hT"], k + 1)
                wait(dve, S["csd"], k)
                wait(dve, S["midn"], k - 1)
                dve.tensor_scalar(cnt_any[:, s], hTc[:, NT * P:NT * P + NT], 1.0, None, ALU.min).then_inc(S["some"], 1)
                dve.tensor_scalar(cnt1[:], hTc[:, NT * P:NT * P + NT], 1.0, None, ALU.max).then_inc(S["any"], 1)

            def count_inv(S, i, s):
                k = 2 * i + s
                dve.wait_ge(S["any"], k + 1)
                wait(dve, S["midc"], k)
                dve.reciprocal(inv_cnt[:], cnt1[:]).then_inc(S["cnt"], 1)

            def mid_sum(S, i, s):
                k = 2 * i + s
                dve.wait_ge(S["cnt"], k + 1)
                dve.wait_ge(S["prec"], k + 1)
                wait(dve, S["midn"], k)
                for j in range(NT):
                    last = dve.scalar_tensor_tensor(out=mid[:, j], in0=p_agg[:, j * F:(j + 1) * F], scalar=inv_cnt[:, j:j + 1],
                                                    in1=pre[:, j], op0=ALU.mult, op1=ALU.add)
                last.then_inc(S["midc"], 1)

            def mid_stats(S, i, s):
                k = 2 * i + s
                dve.wait_ge(S["midc"], k + 1)
                wait(dve, S["midv"], k)
                for j in range(NT):
                    last = dve.bn_stats(stats[:, 1, j], mid[:, j])
                last.then_inc(S["stat1"], 1)

            def mid_scale(S, i, s):
                k = 2 * i + s
                dve.wait_ge(S["csd"], k + 1)
                dve.wait_ge(S["msd"], k + 1)
                wait(dve, S["midn"], k)
                dve.reciprocal(inv_sd[:], cnt_sd[:])
                dve.reciprocal(rstd[:, 1], sd[:, 1]).then_inc(S["rstd1"], 1)

            def mid_norm(S, i, s):
                k = 2 * i + s
                dve.wait_ge(S["rstd1"], k + 1)
                dve.wait_ge(S["some"], k + 1)
                wait(dve, S["mT"], k)
                dve.tensor_tensor(deg_is[:, bass.ds(k * NT, NT)], inv_sd[:], cnt_any[:, s], ALU.mult)
                for j in range(NT):
                    last = dve.tensor_scalar(midn[:, j], mid[:, j], mv[:, 1, j, 0:1], rstd[:, 1, j:j + 1], ALU.subtract, ALU.mult)
                last.then_inc(S["midn"], 1)

            def x1_sum(S, i, s):
                k = 2 * i + s
                dve.wait_ge(S["out"], k + 1)
                dve.wait_ge(S["xb_in"][s], i * 16 + (16 * NT if isinstance(k, int) and k == NK - 1 else 16))
                wait(dve, S["x1_stored"][s], i * 16)
                wait(dve, S["h2"], k - 1)
                dve.tensor_tensor(x1[:, s], p_out.rearrange("p (j h) -> p j h", j=NT), xb[s], ALU.add).then_inc(S["x1c"], 1)

            def x1_stats(S, i, s):
                k = 2 * i + s
                dve.wait_ge(S["x1c"], k + 1)
                wait(dve, S["x1v"], k)
                for j in range(NT):
                    last = dve.bn_stats(stats[:, 2, j], x1[:, s, j])
                last.then_inc(S["stat2"], 1)

            def x1_scale(S, i, s):
                k = 2 * i + s
                dve.wait_ge(S["x1sd"], k + 1)
                wait(dve, S["scale2"], k)
                dve.reciprocal(rstd[:, 2], sd[:, 2]).then_inc(S["rstd2"], 1)

            def h2_scale(S, i, s):
                k = 2 * i + s
                dve.wait_ge(S["midn"], k + 1)
                dve.wait_ge(S["rstd2"], k + 1)
                wait(dve, S["h2"], k)
                dve.tensor_tensor(scale2[:], rstd[:, 2], deg_is[:, bass.ds(k * NT, NT)], ALU.mult).then_inc(S["scale2"], 1)

            def h2_shift(S, i, s):
                k = 2 * i + s
                dve.wait_ge(S["scale2"], k + 1)
                dve.scalar_tensor_tensor(out=nb[:, 2], in0=mv[:, 2, :, 0], scalar=-1.0, in1=scale2[:], op0=ALU.mult, op1=ALU.mult).then_inc(S["x1nb"], 1)

            step_ops = [(2, x_stats), (3, aggregate(0, "stat0", "var", "sd", "nb")), (5, x_scale), (6, x_shift),
                        (12, count_max), (13, count_inv), (16, mid_sum), (17, mid_stats), (18, aggregate(1, "stat1", "midv", "msd", "midn")),
                        (20, mid_scale), (21, mid_norm),
                        (31, x1_sum), (32, x1_stats), (33, aggregate(2, "stat2", "x1v", "x1sd", "x1nb")), (35, x1_scale), (36, h2_scale), (37, h2_shift)]


            dve.wait_ge(s_acc0, 1)
            run(dve, [(1, lower), (0, one_hot(0)), (6, load_nodes(3)), (6, add_window(0))], step_ops, S1)
            with dve.If(general(dve) > 0):
                dve.wait_ge(s_add[0], NG)
                pass_over(dve, S1)
                general_sums(0)
                run(dve, [], step_ops, S2)
                pass_over(dve, S2)
            pass_over(dve, S1)

            def result(S, i, s):
                k = 2 * i + s
                dve.wait_ge(S["turned"], k + 1)
                dve.wait_ge(S["x1_in"][s], i * 16 + 16)
                wait(dve, S["stored"][s], i * 16)
                for j in range(NT):
                    last = dve.scalar_tensor_tensor(out=x1[:, s, j], in0=(p_hT, p_mT)[s][:, j * P:(j + 1) * P],
                                                    scalar=deg_is[:, bass.ds(k * NT + j, 1)], in1=xb[s][:, j], op0=ALU.mult, op1=ALU.add)
                last.then_inc(S["added"], 1)

            run(dve, [(0, one_hot(1)), (2, load_nodes(1)), (2, add_window(1))], [(5, result)], R1)
            with dve.If(general(dve) > 0):
                dve.wait_ge(s_add[1], NG)
                result_over(dve, R1)
                general_sums(1)
                run(dve, [], [(5, result)], R2)


_INS = ['x', 'src', 'dst', 'edge_attr_128', 'L0_gnn_W1', 'L0_gnn_b1', 'L0_gnn_gamma', 'L0_gnn_beta', 'L0_gnn_prelu_a', 'L0_gnn_W2', 'L0_gnn_b2']


def kernel(**inputs):
    import numpy as _np
    import concourse.bacc as _bacc
    from concourse import mybir as _mybir
    from concourse.bass_utils import run_bass_kernel_spmd as _run

    nc = _bacc.Bacc("TRN2", target_bir_lowering=False, num_devices=1)
    arrays, args = {}, []
    for name in _INS:
        a = _np.ascontiguousarray(inputs[name])
        arrays[f"in_{name}_dram"] = a
        args.append(nc.dram_tensor(f"in_{name}_dram", a.shape, _mybir.dt.from_np(a.dtype), kind="ExternalInput").ap())
    n, h = inputs['x'].shape
    padded = -(-n // (NT * P)) * NT * P
    args.append(nc.dram_tensor("table", (padded, h), F32, kind="Internal").ap())
    args.append(nc.dram_tensor("x1_dram", (padded, h), F32, kind="Internal").ap())
    args.append(nc.dram_tensor("out_0_dram", (n, h), F32, kind="ExternalOutput").ap())
    gnn_kernel(nc, *args)
    r = _run(nc, [arrays], core_ids=[0])
    return r.results[0]["out_0_dram"]
```
